# Optimizing a Trainium2 kernel written in Bass

```python
import numpy as np
import jax
import jax.numpy as jnp

def _softmax(x, axis=-1):
    return jax.nn.softmax(x, axis=axis)

def _gelu(x):
    return jax.nn.gelu(x, approximate=True)

def _silu(x):
    return jax.nn.silu(x)

def _sigmoid(x):
    return jax.nn.sigmoid(x)

def _layernorm(x, axis=-1, eps=1e-05):
    m = jnp.mean(x, axis=axis, keepdims=True)
    v = jnp.var(x, axis=axis, keepdims=True)
    return (x - m) / jnp.sqrt(v + eps)

def _scatter_add(tgt, idx, src, axis=0):
    return tgt.at[idx].add(src)

def _segment_sum(src, seg, n):
    return jax.ops.segment_sum(src, seg, n)
kernel_name = 'mk_gnn_ffn_d2_gnn_r8_d5bbea'

def setup_inputs(seed: int=0):
    np.random.seed(seed)
    _w = jnp.asarray

    def _rec_inputs():
        import jax
        import jax.numpy as jnp
        _gk = jax.random.key(seed)
        x = 7.22e-05 + 1 * jax.random.normal(jax.random.fold_in(_gk, 1), (1250, 512), jnp.float32)
        _s = jax.random.randint(jax.random.fold_in(_gk, 2), (10000,), 0, 1250, jnp.int32)
        _d = jax.random.randint(jax.random.fold_in(_gk, 3), (10000,), 0, 1250, jnp.int32)
        _loop = jnp.arange(1250, dtype=jnp.int32)
        src = jnp.concatenate([_s, _d, _loop])
        dst = jnp.concatenate([_d, _s, _loop])
        _o = jnp.argsort(dst, stable=True)
        src = src[_o]
        dst = dst[_o]
        edge_attr_20 = 0.000389844 + 1.00025 * jax.random.normal(jax.random.fold_in(_gk, 12), (21250, 20), jnp.float32)
        edge_attr_4 = -0.00185629 + 0.998788 * jax.random.normal(jax.random.fold_in(_gk, 13), (21250, 4), jnp.float32)
        edge_weight = jax.random.uniform(jax.random.fold_in(_gk, 15), (21250,), jnp.float32, 0.0, 0.999993)
        return (x, src, dst, edge_attr_20, edge_attr_4, edge_weight)
    x, src, dst, edge_attr_20, edge_attr_4, edge_weight = _rec_inputs()

    def _L0_gnn_setup():
        import jax, jax.numpy as jnp
        import numpy as np
        import math
        B = 128
        F = 32
        R = 20
        N = 2048
        E = 32768
        LOG2 = 0.6931471805599453
        IS2 = 1.0 / math.sqrt(2.0)
        IS3 = 1.0 / math.sqrt(3.0)
        IS6 = 1.0 / math.sqrt(6.0)

        def ssp(x):
            return jax.nn.softplus(x) - LOG2
        key = jax.random.key(seed)
        ks = jax.random.split(key, 14)
        return dict(x=jax.random.normal(ks[0], (N, 4 * B), jnp.float32), idx_i=jax.random.randint(ks[1], (E,), 0, N), idx_j=jax.random.randint(ks[2], (E,), 0, N), f_ij=jax.random.normal(ks[3], (E, R), jnp.float32), rcut_ij=jax.random.uniform(ks[4], (E,), jnp.float32), Yr_ij=jax.random.normal(ks[5], (E, 4), jnp.float32), w_in2f_s=jax.random.normal(ks[6], (B, F), jnp.float32), w_in2f_v=jax.random.normal(ks[7], (B, F), jnp.float32), W1=jax.random.normal(ks[8], (R, F), jnp.float32) / math.sqrt(R), b1=jnp.zeros((F,), jnp.float32), W2=jax.random.normal(ks[9], (F, 6 * F), jnp.float32) / math.sqrt(F), b2=jnp.zeros((6 * F,), jnp.float32), w_f2o1_s=jax.random.normal(ks[10], (2 * F, B), jnp.float32), w_f2o1_v=jax.random.normal(ks[11], (2 * F, B), jnp.float32), w_f2o2_s=jax.random.normal(ks[12], (B, B), jnp.float32), w_f2o2_v=jax.random.normal(ks[13], (B, B), jnp.float32))
    _L0_gnn_all = _L0_gnn_setup()
    _L0_gnn_in = {k: v for k, v in _L0_gnn_all.items() if k in ('w_in2f_s', 'w_in2f_v', 'W1', 'b1', 'W2', 'b2', 'w_f2o1_s', 'w_f2o1_v', 'w_f2o2_s', 'w_f2o2_v')}
    del _L0_gnn_all

    def _L0_ffn_setup():
        import jax, jax.numpy as jnp
        import numpy as np
        CAPACITY_FACTOR = 1.2
        key = jax.random.key(seed)
        k1, k2, k3 = jax.random.split(key, 3)
        B, S, D, E = (8, 512, 512, 16)
        x = jax.random.normal(k1, (B, S, D), dtype=jnp.float32)
        switch_w = jax.random.normal(k2, (E, D), dtype=jnp.float32) * 0.02
        switch_b = jnp.zeros((E,), dtype=jnp.float32)
        expert_w = jax.random.normal(k3, (E, D, D), dtype=jnp.float32) * 0.02
        expert_b = jnp.zeros((E, D), dtype=jnp.float32)
        return {'x': x, 'switch_w': switch_w, 'switch_b': switch_b, 'expert_w': expert_w, 'expert_b': expert_b}
    _L0_ffn_all = _L0_ffn_setup()
    _L0_ffn_in = {k: v for k, v in _L0_ffn_all.items() if k in ('switch_w', 'switch_b', 'expert_w', 'expert_b')}
    del _L0_ffn_all

    def _L1_gnn_setup():
        import jax, jax.numpy as jnp
        import numpy as np
        N = 1250
        E = 20000
        C_IN = 512
        C_H = 512

        def _gcn_conv(x, W, b, src, dst, n):
            h = x @ W
            deg = jnp.zeros((n,), x.dtype).at[dst].add(1.0)
            dis = jax.lax.rsqrt(jnp.maximum(deg, 1.0))
            norm = dis[src] * dis[dst]
            msg = h[src] * norm[:, None]
            out = jax.ops.segment_sum(msg, dst, num_segments=n)
            return out + b
        key = jax.random.key(seed)
        ks = jax.random.split(key, 4)
        x = jax.random.normal(ks[0], (N, C_IN), dtype=jnp.float32)
        edge_index = jax.random.randint(ks[1], (2, E), 0, N, dtype=jnp.int64)
        W1 = jax.random.normal(ks[2], (C_IN, C_H), dtype=jnp.float32) / np.float32(np.sqrt(C_IN))
        b1 = jnp.zeros((C_H,), dtype=jnp.float32)
        W2 = jax.random.normal(ks[3], (C_H, C_H), dtype=jnp.float32) / np.float32(np.sqrt(C_H))
        b2 = jnp.zeros((C_H,), dtype=jnp.float32)
        return {'x': x, 'edge_index': edge_index, 'W1': W1, 'b1': b1, 'W2': W2, 'b2': b2}
    _L1_gnn_all = _L1_gnn_setup()
    _L1_gnn_in = {k: v for k, v in _L1_gnn_all.items() if k in ('W1', 'b1', 'W2', 'b2')}
    del _L1_gnn_all

    def _L1_ffn_setup():
        import jax, jax.numpy as jnp
        import numpy as np
        TOP_K = 2
        key = jax.random.key(seed)
        k1, k2, k3, k4 = jax.random.split(key, 4)
        B, S, D, F, E = (4, 512, 512, 256, 16)
        hidden_states = jax.random.normal(k1, (B, S, D), dtype=jnp.float32)
        gate_weight = jax.random.normal(k2, (E, D), dtype=jnp.float32) * 0.02
        w1 = jax.random.normal(k3, (E, F, D), dtype=jnp.float32) * 0.02
        w2 = jax.random.normal(k4, (E, D, F), dtype=jnp.float32) * 0.02
        return {'hidden_states': hidden_states, 'gate_weight': gate_weight, 'w1': w1, 'w2': w2}
    _L1_ffn_all = _L1_ffn_setup()
    _L1_ffn_in = {k: v for k, v in _L1_ffn_all.items() if k in ('gate_weight', 'w1', 'w2')}
    del _L1_ffn_all
    return {'x': x, 'src': src, 'dst': dst, 'edge_attr_20': edge_attr_20, 'edge_attr_4': edge_attr_4, 'edge_weight': edge_weight, 'L0_gnn_w_in2f_s': _L0_gnn_in['w_in2f_s'], 'L0_gnn_w_in2f_v': _L0_gnn_in['w_in2f_v'], 'L0_gnn_W1': _L0_gnn_in['W1'], 'L0_gnn_b1': _L0_gnn_in['b1'], 'L0_gnn_W2': _L0_gnn_in['W2'], 'L0_gnn_b2': _L0_gnn_in['b2'], 'L0_gnn_w_f2o1_s': _L0_gnn_in['w_f2o1_s'], 'L0_gnn_w_f2o1_v': _L0_gnn_in['w_f2o1_v'], 'L0_gnn_w_f2o2_s': _L0_gnn_in['w_f2o2_s'], 'L0_gnn_w_f2o2_v': _L0_gnn_in['w_f2o2_v'], 'L0_ffn_switch_w': _L0_ffn_in['switch_w'], 'L0_ffn_switch_b': _L0_ffn_in['switch_b'], 'L0_ffn_expert_w': _L0_ffn_in['expert_w'], 'L0_ffn_expert_b': _L0_ffn_in['expert_b'], 'L1_gnn_W1': _L1_gnn_in['W1'], 'L1_gnn_b1': _L1_gnn_in['b1'], 'L1_gnn_W2': _L1_gnn_in['W2'], 'L1_gnn_b2': _L1_gnn_in['b2'], 'L1_ffn_gate_weight': _L1_ffn_in['gate_weight'], 'L1_ffn_w1': _L1_ffn_in['w1'], 'L1_ffn_w2': _L1_ffn_in['w2']}

def reference(x, src, dst, edge_attr_20, edge_attr_4, edge_weight, L0_gnn_w_in2f_s, L0_gnn_w_in2f_v, L0_gnn_W1, L0_gnn_b1, L0_gnn_W2, L0_gnn_b2, L0_gnn_w_f2o1_s, L0_gnn_w_f2o1_v, L0_gnn_w_f2o2_s, L0_gnn_w_f2o2_v, L0_ffn_switch_w, L0_ffn_switch_b, L0_ffn_expert_w, L0_ffn_expert_b, L1_gnn_W1, L1_gnn_b1, L1_gnn_W2, L1_gnn_b2, L1_ffn_gate_weight, L1_ffn_w1, L1_ffn_w2):
    import jax
    import jax.numpy as jnp

    def _L0_gnn_ref(x, idx_i, idx_j, f_ij, rcut_ij, Yr_ij, w_in2f_s, w_in2f_v, W1, b1, W2, b2, w_f2o1_s, w_f2o1_v, w_f2o2_s, w_f2o2_v):
        import jax, jax.numpy as jnp
        import numpy as np
        import math
        B = 128
        F = 32
        R = 20
        N = 2048
        E = 32768
        LOG2 = 0.6931471805599453
        IS2 = 1.0 / math.sqrt(2.0)
        IS3 = 1.0 / math.sqrt(3.0)
        IS6 = 1.0 / math.sqrt(6.0)

        def ssp(x):
            return jax.nn.softplus(x) - LOG2
        n = x.shape[0]
        xs = x[:, :B]
        xv = x[:, B:].reshape(n, B, 3)
        hs = xs @ w_in2f_s / math.sqrt(B)
        hv = jnp.einsum('nbc,bf->nfc', xv, w_in2f_v) / math.sqrt(B)
        s = hs[idx_j]
        v = hv[idx_j]
        ys = Yr_ij[:, 0]
        yv = Yr_ij[:, 1:4]
        t_s1 = s * ys[:, None]
        t_s2 = jnp.einsum('efc,ec->ef', v, yv) * IS3
        t_v1 = s[:, :, None] * yv[:, None, :]
        t_v2 = v * ys[:, None, None]
        t_pv = jnp.cross(v, yv[:, None, :]) * IS2
        ax, ay, az = (v[..., 0], v[..., 1], v[..., 2])
        bx, by, bz = (yv[:, None, 0:1], yv[:, None, 1:2], yv[:, None, 2:3])
        bx, by, bz = (bx[..., 0], by[..., 0], bz[..., 0])
        t_q = jnp.stack([(ax * by + ay * bx) * IS2, (ay * bz + az * by) * IS2, (2.0 * az * bz - ax * bx - ay * by) * IS6, (ax * bz + az * bx) * IS2, (ax * bx - ay * by) * IS2], axis=-1)
        h = ssp(f_ij @ W1 + b1)
        Wij = (h @ W2 + b2) * rcut_ij[:, None]
        Wf = Wij.reshape(-1, F, 6)
        edge = jnp.concatenate([(t_s1 * Wf[..., 0])[..., None], (t_s2 * Wf[..., 1])[..., None], t_v1 * Wf[..., 2:3], t_v2 * Wf[..., 3:4], t_pv * Wf[..., 4:5], t_q * Wf[..., 5:6]], axis=-1)
        agg = jax.ops.segment_sum(edge.reshape(edge.shape[0], -1), idx_i, num_segments=n).reshape(n, F, 16)
        s_in = jnp.concatenate([agg[..., 0], agg[..., 1]], axis=1)
        v_in = jnp.concatenate([agg[..., 2:5], agg[..., 5:8]], axis=1)
        os1 = s_in @ w_f2o1_s / math.sqrt(2 * F)
        ov1 = jnp.einsum('nmc,mb->nbc', v_in, w_f2o1_v) / math.sqrt(2 * F)
        os1 = ssp(os1)
        os2 = os1 @ w_f2o2_s / math.sqrt(B)
        ov2 = jnp.einsum('nbc,bd->ndc', ov1, w_f2o2_v) / math.sqrt(B)
        return jnp.concatenate([os2, ov2.reshape(n, -1)], axis=-1)

    def _L0_ffn_ref(x, switch_w, switch_b, expert_w, expert_b):
        import jax, jax.numpy as jnp
        import numpy as np
        CAPACITY_FACTOR = 1.2
        B, S, D = x.shape
        E = switch_w.shape[0]
        N = B * S
        xf = x.reshape(N, D)
        logits = xf @ switch_w.T + switch_b
        probs = jax.nn.softmax(logits, axis=-1)
        route_probs = jnp.max(probs, axis=-1)
        routes = jnp.argmax(probs, axis=-1)
        oh = jax.nn.one_hot(routes, E, dtype=jnp.int32)
        pos = jnp.take_along_axis(jnp.cumsum(oh, axis=0), routes[:, None], axis=1)[:, 0] - 1
        capacity = int(CAPACITY_FACTOR * N / E)
        keep = pos < capacity
        buf = jnp.zeros((E, capacity, D), dtype=xf.dtype).at[routes, pos].set(xf)
        y = jnp.einsum('ecd,efd->ecf', buf, expert_w) + expert_b[:, None, :]
        gathered = y[routes, jnp.minimum(pos, capacity - 1)]
        out = jnp.where(keep[:, None], gathered, xf) * route_probs[:, None]
        return out.reshape(B, S, D)

    def _L1_gnn_ref(x, edge_index, W1, b1, W2, b2):
        import jax, jax.numpy as jnp
        import numpy as np
        N = 1250
        E = 20000
        C_IN = 512
        C_H = 512

        def _gcn_conv(x, W, b, src, dst, n):
            h = x @ W
            deg = jnp.zeros((n,), x.dtype).at[dst].add(1.0)
            dis = jax.lax.rsqrt(jnp.maximum(deg, 1.0))
            norm = dis[src] * dis[dst]
            msg = h[src] * norm[:, None]
            out = jax.ops.segment_sum(msg, dst, num_segments=n)
            return out + b
        n = x.shape[0]
        loops = jnp.arange(n, dtype=edge_index.dtype)
        src = jnp.concatenate([edge_index[0], loops])
        dst = jnp.concatenate([edge_index[1], loops])
        h = _gcn_conv(x, W1, b1, src, dst, n)
        h = jax.nn.relu(h)
        return _gcn_conv(h, W2, b2, src, dst, n)

    def _L1_ffn_ref(hidden_states, gate_weight, w1, w2):
        import jax, jax.numpy as jnp
        import numpy as np
        TOP_K = 2
        B, S, D = hidden_states.shape
        E = gate_weight.shape[0]
        x = hidden_states.reshape(-1, D)
        gate_logits = x @ gate_weight.T
        top_vals, top_idx = jax.lax.top_k(gate_logits, TOP_K)
        routing_w = jax.nn.softmax(top_vals, axis=-1)
        mask = jnp.any(top_idx[:, :, None] == jnp.arange(E)[None, None, :], axis=1)
        h = jax.nn.silu(jnp.einsum('td,efd->tef', x, w1))
        counts = jnp.sum(mask, axis=0)
        h_sum = jnp.einsum('tef,te->ef', h, mask.astype(h.dtype))
        h_mean = h_sum / jnp.maximum(counts, 1)[:, None].astype(h.dtype)
        y_mean = jnp.einsum('ef,edf->ed', h_mean, w2)
        y_mean = jnp.where((counts > 0)[:, None], y_mean, 0.0)
        out = jnp.einsum('tk,tkd->td', routing_w, y_mean[top_idx])
        return out.reshape(B, S, D)
    edge_index = jnp.stack([src, dst])
    x = x + _L0_gnn_ref(_layernorm(x, axis=-1), src, dst, edge_attr_20, edge_weight, edge_attr_4, L0_gnn_w_in2f_s, L0_gnn_w_in2f_v, L0_gnn_W1, L0_gnn_b1, L0_gnn_W2, L0_gnn_b2, L0_gnn_w_f2o1_s, L0_gnn_w_f2o1_v, L0_gnn_w_f2o2_s, L0_gnn_w_f2o2_v)
    x = x + _L0_ffn_ref(_layernorm(x, axis=-1)[None], L0_ffn_switch_w, L0_ffn_switch_b, L0_ffn_expert_w, L0_ffn_expert_b)[0]
    x = x + _L1_gnn_ref(_layernorm(x, axis=-1), edge_index, L1_gnn_W1, L1_gnn_b1, L1_gnn_W2, L1_gnn_b2)
    x = x + _L1_ffn_ref(_layernorm(x, axis=-1)[None], L1_ffn_gate_weight, L1_ffn_w1, L1_ffn_w2)[0]
    return x

_drawn_inputs = setup_inputs


def setup_inputs(seed=0):
    import zlib

    import numpy as np

    out = dict(_drawn_inputs(seed))
    spreads = {'L0_gnn_b1': (0.0, 0.1),
     'L0_gnn_b2': (0.0, 0.1),
     'L0_ffn_switch_b': (0.0, 0.1),
     'L0_ffn_expert_b': (0.0, 0.73),
     'L1_gnn_b1': (0.0, 0.1),
     'L1_gnn_b2': (0.0, 0.1)}
    factors = {'L1_ffn_gate_weight': 6.214, 'L1_ffn_w1': 8.0, 'L1_ffn_w2': 5.911}
    for name, (base, spread) in spreads.items():
        noise = np.random.default_rng([zlib.crc32(name.encode()), seed]).standard_normal(out[name].shape)
        drawn = base * np.exp(spread * noise) if base else spread * noise
        out[name] = jnp.asarray(drawn.astype(out[name].dtype))
    for name, factor in factors.items():
        out[name] = (out[name] * factor).astype(out[name].dtype)
    return out
```

```python
from contextlib import ExitStack
import math

import concourse.bass as bass
from concourse import mybir

F32, BF16, F16, I32 = mybir.dt.float32, mybir.dt.bfloat16, mybir.dt.float16, mybir.dt.int32
ALU, ACT, AX = mybir.AluOpType, mybir.ActivationFunctionType, mybir.AxisListType
ds = bass.ds

N, D, E = 1250, 512, 21250
TN, NT = 125, 10
B, F, R = 128, 32, 20
NE = 168
NQ = NE // 4
PAD = 2000
SLOTS = 176
RD = 8
CH = 384
NCH = NQ * 128 // CH
LOG2 = 0.6931471805599453
IS3 = 1.0 / math.sqrt(3.0)
R_D, R_S, R_I, REC = 256, 257, 258, 260
KC = D // 128
NX = 16
CAP = int(1.2 * N / NX)
H1 = 256
JOBS = 36
PU = 5
JU = 6


class Steps:

    def __init__(self, eng, sem):
        self.eng, self.sem, self.n = eng, sem, 0

    def mark(self, ins):
        ins.then_inc(self.sem, 1)
        self.n += 1

    def wait(self):
        self.eng.wait_ge(self.sem, self.n)

    def __call__(self, ins):
        self.mark(ins)
        self.wait()


def edge_phase(nc, P, A, X, agg, PS, x, fT_d, sm_d, ds_i, w2e, b2e, in2f_s, in2f_v, W1, b1, zero_rows):
    ctx = ExitStack()

    def sb(name, shape, dt=F32):
        return ctx.enter_context(nc.sbuf_tensor(name, shape, dt))

    def sem(name):
        return ctx.enter_context(nc.semaphore(name))

    with ctx:
        hv_dram = nc.dram_tensor("hv_dram", (N, 6 * F), F32, kind="Internal").ap()
        rec_dram = nc.dram_tensor("rec_dram", (SLOTS * 128, REC), F32, kind="Internal").ap()
        xn = sb("xn", [TN, D])
        stats, mv = P["stats"], sb("mv", [TN, NT, 2])
        var, rstd, rtmp = sb("var", [TN, NT]), sb("rstd", [TN, NT]), sb("rtmp", [TN, NT])
        ident, ones, before = P["ident"], P["ones"], P["before"]
        iota_f, iota_h = P["asum"], sb("iota_h", [128, N], F16)
        ws = sb("ws", [128, 2, F])
        wt = sb("wt", [128, 4, 128])
        xv, hvs = sb("xv", [128, 4, TN]), sb("hvs", [TN, 3, 2, F])
        w1b, b1c = sb("w1b", [4 * R, 128]), sb("b1c", [128, 1])
        w2b, b2r = sb("w2b", [128, 4, 128]), sb("b2r", [128, 128])
        fT = A[0:4 * R, 0:5, :].rearrange("p a b -> p (a b)")[:, 0:NQ * 128]
        zr = sb("zr", [128, NQ * 128])
        hp, hq = sb("hp", [128, NQ * 128]), sb("hq", [128, 2, 128])
        sm, smi = sb("small", [128, NE, 6]), sb("smi", [128, 2, NE], I32)
        yy = sb("yy", [128, NE, 5])
        sf = sb("sf", [128, NE])
        ge, oh, sc = sb("ge", [128, 12, NE]), sb("oh", [128, 11, NE]), sb("sc", [128, 11, NE])
        pos, ptmp, posI = sb("pos", [128, NE]), sb("ptmp", [128, NE]), sb("posI", [128, NE], I32)
        cnt, off, nb, nbi = sb("cnt", [128, 11]), sb("off", [128, 11]), sb("nb", [128, 8, 11]), sb("nbi", [128, 6, 11], I32)
        zb, zt = sb("zb", [128, 512], BF16), sb("zt", [128, 512])
        BB, TB, btmp = sb("BB", [128, SLOTS + 1]), sb("TB", [128, SLOTS + 1]), sb("btmp", [128, SLOTS + 1])
        B125, meta = sb("B125", [128, SLOTS]), sb("meta", [1, 2, SLOTS + 1], I32)
        pl, ir = sb("pl", [128, 8, REC]), sb("ir", [128, 8], I32)
        pt_rec = hp[:, 0:RD * REC].rearrange("p (k r) -> p k r", k=RD)
        G = hp[:, RD * REC:RD * (REC + 6 * F)].rearrange("p (k r) -> p k r", k=RD)
        M = zr[:, 0:4 * 320].rearrange("p (q m) -> p q m", q=4)
        oD = zr[:, 4 * 320:4 * 320 + 2 * N].bitcast(BF16).rearrange("p (q n) -> p q n", q=4)
        sl = sb("sl", [128, RD])
        oB, oF = sb("oB", [128, 4, TN], BF16), sb("oF", [128, 4, TN])
        dist = sb("dist", [128, 4, TN])

        pz, pw, pt = PS[:, 0:2, :], PS[:, 2:4, :], PS[:, 4, :]
        pg, pm = PS[:, 5:8, :], PS[:, 4, 0:320]

        S = {n: sem(n) for n in """x_in w1_in w_in edge_in f_in const_ok dve_step pool_step act_step xn_ready xn_free xT_ready xv_ready
            hv_mm hv_ready hv_out hvs_free sm_ok cnt_ok cnt_mm pos_ok meta_ok pads_ok iota_ok var_ok std_ok
            z_mm z_act z_ln z_h zero_ok hq_ok w_mm evac_ok small_ok rec_pad full_ok zeros_out
            rec_ok oneh_ok dist_ok ohf_ok msg_ok agg_mm copied sent flushed """.split()}
        scat = [P["sems"].enter_context(nc.semaphore(f"scat{k}")) for k in range(8)]
        rin = [sem(f"rin{k}") for k in range(RD)]
        gat = [P["sems"].enter_context(nc.semaphore(f"gat{k}")) for k in range(RD)]
        edges = ExitStack()
        block = edges.enter_context(nc.Block())

        @block.sync
        def _(sp):
            sp.dma_start(smi[:, :, :], ds_i).then_inc(S["edge_in"], 16)
            sp.wait_ge(S["const_ok"], 2)
            for g in range(4):
                sp.dma_start(w1b[R * g:R * g + R, F * g:F * g + F], W1).then_inc(S["w1_in"], 16)
                sp.dma_start(b1c[F * g:F * g + F, :], b1).then_inc(S["w1_in"], 16)
            sp.dma_start(yy[:, :, :], sm_d).then_inc(S["edge_in"], 16)
            for g in range(4):
                sp.dma_start(w2b[F * g:F * g + F, g, :], w2e).then_inc(S["w_in"], 16)
            sp.dma_start(b2r[:, :], b2e.broadcast_to([128, 128])).then_inc(S["w_in"], 16)
            sp.dma_start(ws[:, 0, :], in2f_s).then_inc(S["w_in"], 16)
            sp.dma_start(ws[:, 1, :], in2f_v).then_inc(S["w_in"], 16)
            sp.sem_inc(S["hvs_free"], 1)
            sp.wait_ge(S["pads_ok"], 3)
            sp.dma_start(rec_dram[NE * 128:SLOTS * 128, :].rearrange("(p q) r -> p q r", q=8), pl[:, :, :]).then_inc(S["rec_pad"], 16)
            for rows in zero_rows:
                n, q = rows.shape[0], rows.shape[1]
                sp.dma_start(rows, zt[0:n, :].rearrange("p (a d) -> p a d", a=1).broadcast_to([n, q, D])).then_inc(S["zeros_out"], 16)
            with sp.Fori(0, NT) as t:
                sp.wait_ge(S["hv_ready"], t + 1)
                sp.dma_start(hv_dram[ds(t * TN, TN), :], hvs[:, :, :, :].rearrange("p c b f -> p (c b f)")).then_inc(S["hv_out"], 16)
                sp.wait_ge(S["hv_out"], t * 16 + 16)
                sp.sem_inc(S["hvs_free"], 1)
            for k in range(8):
                sp.wait_ge(scat[k], 16 * (NE // 8))
            sp.wait_ge(S["meta_ok"], 1)
            with sp.Fori(0, SLOTS // RD) as i:
                for k in range(RD):
                    t = sp.value_load(meta[0:1, 0, ds(i * RD + k, 1)], min_val=0, max_val=SLOTS - 1)
                    sp.wait_ge(S["msg_ok"], i * RD + (k + 1))
                    sp.dma_start(pt_rec[:, k, :], rec_dram[ds(t * 128, 128), :]).then_inc(rin[k], 16)
            sp.wait_ge(S["zeros_out"], 16 * len(zero_rows))

        @block.gpsimd
        def _(pool):
            step = Steps(pool, S["pool_step"])
            pool.memset(w1b[:, :], 0.0).then_inc(S["const_ok"], 1)
            pool.memset(w2b[:, :, :], 0.0).then_inc(S["const_ok"], 1)
            pool.memset(ones[:, :], 1.0).then_inc(S["const_ok"], 1)
            step.mark(pool.memset(ident[:, :], 0.0))
            step.mark(pool.memset(before[:, :], 1.0))
            step.wait()
            pool.affine_select(out=ident[:, :], in_=ident[:, :], compare_op=ALU.not_equal, fill=1.0, base=0,
                               pattern=[[-1, 128]], channel_multiplier=1).then_inc(S["const_ok"], 1)
            pool.affine_select(out=before[:, :], in_=before[:, :], compare_op=ALU.is_gt, fill=0.0, base=0,
                               pattern=[[1, 128]], channel_multiplier=-1).then_inc(S["const_ok"], 1)
            pool.iota(iota_f[:, :], [[1, N]], base=0, channel_multiplier=0, allow_small_or_imprecise_dtypes=True).then_inc(S["const_ok"], 1)
            step(pool.memset(pl[:, :, :], 0.0))
            pool.memset(pl[:, :, R_S:R_S + 1], float(PAD)).then_inc(S["pads_ok"], 1)
            pool.memset(zb[:, :], 0.0).then_inc(S["pads_ok"], 1)
            pool.memset(zt[:, :], 0.0).then_inc(S["pads_ok"], 1)
            pool.memset(agg[:, :, :], 0.0).then_inc(S["zero_ok"], 1)
            pool.wait_ge(S["pos_ok"], 1)
            with pool.Fori(0, NE // 8) as i:
                for k in range(8):
                    pool.wait_ge(S["small_ok"], i * 8 + (k + 1))
                    pool.wait_ge(S["full_ok"], i * 8 + (k + 5))
                    pool.sem_inc(S["sent"], 1)
                    pool.indirect_dma_start(out=rec_dram, out_offset=bass.IndirectOffsetOnAxis(ap=ir[:, k:k + 1], axis=0),
                                            in_=pl[:, k, :], in_offset=None).then_inc(scat[k], 16)
            pool.wait_ge(S["hv_out"], 16 * NT)
            with pool.Fori(0, SLOTS // RD) as i:
                for k in range(RD):
                    pool.wait_ge(rin[k], i * 16 + 16)
                    pool.wait_ge(S["dist_ok"], i * RD + (k + 1))
                    pool.tensor_tensor(sl[:, k:k + 1], pt_rec[:, k, R_S:R_S + 1], B125[:, ds(i * RD + k, 1)], ALU.subtract).then_inc(S["rec_ok"], 1)
                    pool.indirect_dma_start(out=G[:, k, :], out_offset=None, in_=hv_dram,
                                            in_offset=bass.IndirectOffsetOnAxis(ap=pt_rec[:, k, R_I:R_I + 1].bitcast(I32), axis=0)).then_inc(gat[k], 16)

        @block.scalar
        def _(act):
            step = Steps(act, S["act_step"])
            act.dma_start(fT, fT_d).then_inc(S["f_in"], 16)
            act.dma_start(X[:, :, :], x.rearrange("(t p) d -> p t d", p=TN)).then_inc(S["x_in"], 16)
            act.wait_ge(S["const_ok"], 6)
            act.wait_ge(S["w1_in"], 128)
            for c in range(NCH):
                act.wait_ge(S["z_mm"], c + 1)
                z, at = pz[:, c % 2, 0:CH], slice(c * CH, (c + 1) * CH)
                step.mark(act.activation(hp[:, at], z, ACT.Abs, bias=b1c[:, :]))
                act.activation(zr[:, at], z, ACT.Relu, bias=b1c[:, :]).then_inc(S["z_act"], 1)
                step.wait()
                step.mark(act.activation(hp[:, at], hp[:, at], ACT.Exp, scale=-1.0))
            step.wait()
            for c in range(4):
                at = slice(c * NQ * 32, (c + 1) * NQ * 32)
                act.activation(hp[:, at], hp[:, at], ACT.Ln, bias=ones[:, 0:1]).then_inc(S["z_ln"], 1)
            act.wait_ge(S["z_h"], 4)
            act.wait_ge(S["pos_ok"], 1)
            act.wait_ge(S["pads_ok"], 3)
            act.wait_ge(S["rec_pad"], 16)
            def records(i, first):
                for k in range(8):
                    u, g = k // 4, k % 4
                    if g == 0:
                        act.wait_ge(S["w_mm"], i * 8 + (k + 4))
                        act.activation(hq[:, u, :], hp[:, ds((i * 2 + u) * 128, 128)], ACT.Copy).then_inc(S["hq_ok"], 1)
                    if not first:
                        act.wait_ge(scat[k], i * 16)
                    act.activation(pl[:, k, R_D:R_I], sm[:, ds(i * 8 + k, 1), 4:6].rearrange("p a m -> p (a m)"), ACT.Copy)
                    act.activation(pl[:, k, R_I:R_I + 1].bitcast(I32), smi[:, 1, ds(i * 8 + k, 1)], ACT.Copy)
                    act.activation(ir[:, k:k + 1], posI[:, ds(i * 8 + k, 1)], ACT.Copy).then_inc(S["small_ok"], 1)

            records(0, True)
            act.wait_ge(S["var_ok"], 1)
            act.activation(rstd[:, :], var[:, :], ACT.Sqrt).then_inc(S["std_ok"], 1)
            with act.Fori(1, NE // 8) as i:
                records(i, False)
            act.wait_ge(S["zero_ok"], 1 + NT)
            act.wait_ge(S["meta_ok"], 1)
            act.sem_inc(S["dist_ok"], RD)
            def finish(end, turned, copied):
                with act.If(end > 0):
                    b = nc.s_assert_within(end - 1, 0, NT - 1, skip_runtime_bounds_check_because="inside the branch it is 1 + a node tile")
                    act.wait_ge(S["agg_mm"], turned)
                    for q3, n3, c0 in ((0, 500, 0), (1, 500, 0), (2, 250, 0)):
                        act.activation(A[:, ds(b, 1), 500 * q3:500 * q3 + n3].rearrange("p a m -> p (a m)"), pg[0:TN, q3, c0:c0 + n3], ACT.Copy)
                    act.activation(agg[:, ds(b, 1), :].rearrange("p a m -> p (a m)"), pm[0:TN, :], ACT.Copy).then_inc(S["copied"], 1)
                    act.wait_ge(S["copied"], copied)
                    for q3, n3 in ((0, 500), (1, 500), (2, 250)):
                        act.activation(pg[0:TN, q3, 0:n3], zt[0:TN, 0:n3], ACT.Copy)
                    act.activation(pm[0:TN, :], zt[0:TN, 0:320], ACT.Copy).then_inc(S["copied"], 1)
                    act.wait_ge(S["copied"], copied + 1)
                    act.sem_inc(S["flushed"], 1)
                with act.Else():
                    act.sem_inc(S["copied"], 2)
                    act.sem_inc(S["flushed"], 1)

            with act.Fori(0, SLOTS // RD) as i:
                for k in range(RD):
                    q = k % 4
                    act.wait_ge(S["rec_ok"], i * RD + (k + 1))
                    act.activation(dist[:, q, :], iota_f[:, 0:TN], ACT.Abs, bias=sl[:, k:k + 1], scale=-1.0).then_inc(S["dist_ok"], 1)
                    end = act.value_load(meta[0:1, 1, ds(i * RD + k, 1)], min_val=0, max_val=NT)
                    act.wait_ge(S["agg_mm"], i * RD + (k + 1))
                    act.wait_ge(S["dist_ok"], i * RD + (k + RD + 1))
                    act.activation(oF[:, q, :], dist[:, q, :], ACT.Relu, bias=ones[:, 0:1], scale=-1.0).then_inc(S["ohf_ok"], 1)
                    finish(end, i * RD + (k + 4), i * (2 * RD) + (2 * k + 1))
            end = act.value_load(meta[0:1, 1, SLOTS:SLOTS + 1], min_val=0, max_val=NT)
            finish(end, SLOTS + 4, 2 * SLOTS + 1)

        @block.vector
        def _(dve):
            step = Steps(dve, S["dve_step"])
            dve.sem_inc(S["msg_ok"], RD)
            dve.wait_ge(S["const_ok"], 6)
            step.mark(dve.tensor_copy(iota_h[:, :], iota_f[:, :]))
            dve.wait_ge(S["edge_in"], 32)
            step(dve.tensor_copy(sf[:, :], smi[:, 0, :]))
            for b in range(11):
                step.mark(dve.tensor_scalar(ge[:, b, :], sf[:, :], float(TN * b), None, ALU.is_ge))
            step.mark(dve.memset(ge[:, 11, :], 0.0))
            step.wait()
            step(dve.tensor_tensor(oh[:, :, :], ge[:, 0:11, :], ge[:, 1:12, :], ALU.subtract))
            for b in range(11):
                step.mark(dve.tensor_tensor_scan(out=sc[:, b, :], data0=oh[:, b, :], data1=ge[:, 11, :], initial=0.0, op0=ALU.add, op1=ALU.add))
            step.wait()
            dve.tensor_copy(cnt[:, :], sc[:, :, NE - 1]).then_inc(S["cnt_ok"], 1)
            step.mark(dve.tensor_copy(sm[:, :, 4], smi[:, 1, :]))
            step.mark(dve.tensor_copy(sm[:, :, 5], sf[:, :]))
            step(dve.tensor_tensor(sm[:, :, 0:4], yy[:, :, 0:4], yy[:, :, 4:5].broadcast_to([128, NE, 4]), ALU.mult))
            dve.sem_inc(S["sm_ok"], 1)
            dve.wait_ge(S["cnt_mm"], 1)
            step(dve.tensor_copy(nb[:, 0, :], pt[:, 16:27]))
            step(dve.tensor_tensor_scan(out=nb[:, 7, :], data0=nb[:, 0, :], data1=ge[:, 11, 0:11], initial=0.0, op0=ALU.add, op1=ALU.add))
            step(dve.tensor_tensor(nb[:, 1, :], nb[:, 7, :], nb[:, 0, :], ALU.subtract))
            step(dve.scalar_tensor_tensor(out=off[:, :], in0=nb[:, 1, :], scalar=-1.0, in1=pt[:, 0:11], op0=ALU.add, op1=ALU.add))
            for b in range(11):
                if b == 0:
                    step(dve.scalar_tensor_tensor(out=pos[:, :], in0=sc[:, 0, :], scalar=off[:, 0:1], in1=oh[:, 0, :], op0=ALU.add, op1=ALU.mult))
                else:
                    step(dve.scalar_tensor_tensor(out=ptmp[:, :], in0=sc[:, b, :], scalar=off[:, b:b + 1], in1=oh[:, b, :], op0=ALU.add, op1=ALU.mult))
                    step(dve.tensor_tensor(pos[:, :], pos[:, :], ptmp[:, :], ALU.add))
            step(dve.tensor_copy(posI[:, :], pos[:, :]))
            step(dve.tensor_scalar(nb[:, 2, :], nb[:, 7, :], 127.0, None, ALU.add))
            step.mark(dve.tensor_copy(nbi[:, 0, :], nb[:, 1, :]))
            step.mark(dve.tensor_copy(nbi[:, 1, :], nb[:, 7, :]))
            step(dve.tensor_copy(nbi[:, 2, :], nb[:, 2, :]))
            step(dve.tensor_scalar(nbi[:, 3:6, :], nbi[:, 0:3, :], 7, None, ALU.arith_shift_right))
            step(dve.tensor_copy(nb[:, 3:6, :], nbi[:, 3:6, :]))
            step(dve.tensor_tensor(nb[:, 6, :], nb[:, 5, :], nb[:, 3, :], ALU.subtract))
            step(dve.tensor_tensor(nb[:, 2, :], nb[:, 4, :], nb[:, 5, :], ALU.subtract))
            step(dve.tensor_tensor_scan(out=nb[:, 7, :], data0=nb[:, 6, :], data1=ge[:, 11, 0:11], initial=0.0, op0=ALU.add, op1=ALU.add))
            step.mark(dve.memset(BB[:, :], 0.0))
            step(dve.tensor_copy(TB[:, :], iota_f[:, 0:SLOTS + 1]))

            def pairs(tiles):
                for b in tiles:
                    step.mark(dve.scalar_tensor_tensor(out=BB[:, :], in0=iota_f[:, 0:SLOTS + 1], scalar=nb[:, 7, b:b + 1], in1=BB[:, :], op0=ALU.is_ge, op1=ALU.add))
                    step(dve.tensor_scalar(btmp[:, :], iota_f[:, 0:SLOTS + 1], nb[:, 7, b:b + 1], nb[:, 2, b:b + 1], ALU.is_ge, ALU.mult))
                    step(dve.tensor_tensor(TB[:, :], TB[:, :], btmp[:, :], ALU.add))

            pairs(range(4))
            for c in range(4):
                at = slice(c * NQ * 32, (c + 1) * NQ * 32)
                dve.wait_ge(S["z_ln"], c + 1)
                dve.scalar_tensor_tensor(out=hp[:, at], in0=zr[:, at], scalar=-LOG2, in1=hp[:, at], op0=ALU.add, op1=ALU.add).then_inc(S["z_h"], 1)
            dve.sem_inc(S["pos_ok"], 1)

            dve.sem_inc(S["evac_ok"], 2)
            dve.sem_inc(S["full_ok"], 4)
            dve.wait_ge(S["rec_pad"], 16)
            dve.wait_ge(S["w_in"], 16 * 7)

            def w_bias(i, k):
                dve.wait_ge(S["w_mm"], i * 8 + (k + 9))
                dve.wait_ge(S["full_ok"], i * 8 + (k + 1))
                dve.tensor_tensor(wt[:, k % 4, :], pw[:, k % 2, 0:128], b2r[:, :], ALU.add).then_inc(S["evac_ok"], 1)

            def w_evac(i, first):
                w_bias(i, 0)
                for k in range(8):
                    if k < 7:
                        w_bias(i, k + 1)
                    if not first:
                        dve.wait_ge(scat[k], i * 16)
                    dve.wait_ge(S["evac_ok"], i * 8 + (k + 3))
                    y = sm[:, ds(i * 8 + k, 1), 0:4]
                    dve.tensor_scalar(pl[:, k, 0:64], wt[:, k % 4, 0:64], y[:, :, 0:1].rearrange("p a m -> p (a m)"), None, ALU.mult)
                    dve.tensor_tensor(pl[:, k, 64:256].rearrange("p (c f) -> p c f", c=3), wt[:, k % 4, 64:128].rearrange("p (a f) -> p a f", a=1).broadcast_to([128, 3, 64]),
                                      y[:, :, 1:4].rearrange("p a m -> p m a").broadcast_to([128, 3, 64]), ALU.mult).then_inc(S["full_ok"], 1)

            w_evac(0, True)
            dve.wait_ge(S["x_in"], 16)
            for t in range(NT):
                step.mark(dve.bn_stats(stats[:, t, :], X[:, t, :]))
            step.wait()
            for t in range(NT):
                step.mark(dve.bn_aggr(mv[:, t, :], stats[:, t, :]))
            step.wait()
            step(dve.tensor_scalar(var[:, :], mv[:, :, 1], 1e-5, None, ALU.add))
            dve.sem_inc(S["var_ok"], 1)
            dve.wait_ge(S["std_ok"], 1)
            step(dve.reciprocal(rstd[:, :], rstd[:, :]))
            step(dve.tensor_tensor(rtmp[:, :], rstd[:, :], rstd[:, :], ALU.mult))
            step(dve.tensor_tensor(rtmp[:, :], rtmp[:, :], var[:, :], ALU.mult))
            step(dve.tensor_scalar(rtmp[:, :], rtmp[:, :], -0.5, 1.5, ALU.mult, ALU.add))
            step(dve.tensor_tensor(rstd[:, :], rstd[:, :], rtmp[:, :], ALU.mult))
            with dve.Fori(1, NT + 1) as i:
                w_evac(i, False)
                dve.wait_ge(S["xn_free"], i)
                dve.tensor_scalar(xn[:, :], X[:, ds(i - 1, 1), :].rearrange("p a d -> p (a d)"), mv[:, ds(i - 1, 1), 0:1].rearrange("p a d -> p (a d)"), rstd[:, ds(i - 1, 1)], ALU.subtract, ALU.mult).then_inc(S["xn_ready"], 1)
                dve.wait_ge(S["xT_ready"], i)
                dve.tensor_copy(xv[:, :, :], pt[:, 0:500].rearrange("p (c n) -> p c n", c=4)).then_inc(S["xv_ready"], 1)
                dve.wait_ge(S["hv_mm"], i)
                dve.wait_ge(S["hvs_free"], i)
                dve.tensor_scalar(hvs[:, :, 0, :], pz[0:TN, 0, 0:32].rearrange("p (a f) -> p a f", a=1).broadcast_to([TN, 3, 32]), 1.0 / math.sqrt(B), None, ALU.mult)
                dve.tensor_scalar(hvs[:, :, 1, :], pz[0:TN, 0, 32:128].rearrange("p (c f) -> p c f", c=3), 1.0 / math.sqrt(B), None, ALU.mult).then_inc(S["hv_ready"], 1)
            with dve.Fori(NT + 1, NE // 8) as i:
                w_evac(i, False)
                dve.tensor_scalar(tile(A, i - (NT + 1)), iota_f[0:TN, :], 0.0, None, ALU.mult).then_inc(S["zero_ok"], 1)
            pairs(range(4, NT - 1))
            step.mark(dve.tensor_scalar(B125[:, :], BB[:, 0:SLOTS], float(TN), None, ALU.mult))
            step.mark(dve.tensor_copy(meta[:, 0, 0:SLOTS], TB[0:1, 0:SLOTS]))
            step.mark(dve.memset(meta[:, 1, 0:1], 0))
            step(dve.tensor_tensor(btmp[0:1, 0:SLOTS], BB[0:1, 1:SLOTS + 1], BB[0:1, 0:SLOTS], ALU.not_equal))
            step(dve.memset(btmp[0:1, SLOTS - 1:SLOTS], 1.0))
            step(dve.scalar_tensor_tensor(out=meta[:, 1, 1:SLOTS + 1], in0=BB[0:1, 0:SLOTS], scalar=1.0, in1=btmp[0:1, 0:SLOTS], op0=ALU.add, op1=ALU.mult))
            dve.sem_inc(S["meta_ok"], 1)
            with dve.Fori(0, SLOTS // RD) as i:
                for k in range(RD):
                    q = k % 4
                    rec = pt_rec[:, k, :]
                    dve.wait_ge(S["rec_ok"], i * RD + (k + 1))
                    dve.wait_ge(S["agg_mm"], i * RD + (k + 1))
                    dve.tensor_scalar(oD[:, q, :], iota_h[:, :], rec[:, R_D:R_D + 1], None, ALU.is_equal)
                    dve.tensor_scalar(oB[:, q, :], iota_h[:, 0:TN], sl[:, k:k + 1], None, ALU.is_equal).then_inc(S["oneh_ok"], 1)
                    dve.wait_ge(gat[k], i * 16 + 16)
                    dve.tensor_tensor(M[:, q, 0:32], G[:, k, 0:32], rec[:, 0:32], ALU.mult)
                    dve.tensor_tensor(M[:, q, 32:128].rearrange("p (c f) -> p c f", c=3), G[:, k, :].rearrange("p (c b f) -> p c b f", c=3, b=2)[:, :, 1, :],
                                      rec[:, 32:64].rearrange("p (a f) -> p a f", a=1).broadcast_to([128, 3, 32]), ALU.mult)
                    dve.tensor_tensor(M[:, q, 128:320], G[:, k, :], rec[:, 64:256], ALU.mult).then_inc(S["msg_ok"], 1)

        @block.tensor
        def _(pe):
            pe.wait_ge(S["const_ok"], 6)
            pe.wait_ge(S["w1_in"], 128)
            pe.wait_ge(S["f_in"], 16)
            for c in range(NCH):
                if c >= 2:
                    pe.wait_ge(S["z_act"], c - 1)
                pe.matmul(pz[:, c % 2, 0:CH], w1b[:, :], fT[:, c * CH:(c + 1) * CH], start=True, stop=True).then_inc(S["z_mm"], 1)
                if c == 4:
                    pe.wait_ge(S["cnt_ok"], 1)
                    pe.matmul(pt[:, 0:11], before[:, :], cnt[:, :], start=True, stop=True)
                    pe.matmul(pt[:, 16:27], ones[:, :], cnt[:, :], start=True, stop=True).then_inc(S["cnt_mm"], 1)
            pe.wait_ge(S["w_in"], 16 * 7)
            pe.sem_inc(S["w_mm"], 8)
            pe.sem_inc(S["xn_free"], 1)

            def w_records(i):
                for k in range(8):
                    if k % 4 == 0:
                        pe.wait_ge(S["hq_ok"], i * 2 + (k // 4 + 1))
                    pe.wait_ge(S["evac_ok"], i * 8 + (k + 1))
                    pe.matmul(pw[:, k % 2, 0:128], hq[:, k // 4, :], w2b[:, k % 4, :], start=True, stop=True).then_inc(S["w_mm"], 1)

            w_records(0)
            with pe.Fori(1, NT + 1) as i:
                w_records(i)
                pe.wait_ge(S["xn_ready"], i)
                for c in range(4):
                    v = xn[:, 0:128] if c == 0 else xn[:, 128 + c - 1:D:3]
                    ins = pe.transpose(pt[:, c * TN:c * TN + TN], v, ident[0:TN, 0:TN])
                ins.then_inc(S["xT_ready"], 1)
                pe.wait_ge(S["xT_ready"], i)
                pe.sem_inc(S["xn_free"], 1)
                pe.wait_ge(S["xv_ready"], i)
                for c in range(4):
                    ins = pe.matmul(pz[0:TN, 0, 32 * c:32 * c + 32], xv[:, c, :], ws[:, min(c, 1), :], start=True, stop=True)
                ins.then_inc(S["hv_mm"], 1)
            with pe.Fori(NT + 1, NE // 8) as i:
                w_records(i)
            pe.wait_ge(S["pads_ok"], 3)
            for q in range(3):
                pe.matmul(pg[0:TN, q, :], zb[:, 0:TN], zb[:, :], start=True, stop=True)
            pe.matmul(pm[0:TN, :], zb[:, 0:TN], zb[:, 0:320], start=True, stop=True)
            pe.sem_inc(S["agg_mm"], 4)
            with pe.Fori(0, SLOTS // RD) as i:
                for k in range(RD):
                    q = k % 4
                    pe.wait_ge(S["oneh_ok"], i * RD + (k + 1))
                    pe.wait_ge(S["flushed"], i * RD + (k + 1))
                    for q3, n3, c0 in ((0, 500, 0), (1, 500, 0), (2, 250, 0)):
                        pe.matmul(pg[0:TN, q3, c0:c0 + n3], oB[:, q, :], oD[:, q, 500 * q3:500 * q3 + n3], start=False, stop=True, skip_group_check=True)
                    pe.wait_ge(S["ohf_ok"], i * RD + (k + 1))
                    pe.wait_ge(S["msg_ok"], i * RD + (k + RD + 1))
                    pe.matmul(pm[0:TN, :], oF[:, q, :], M[:, q, :], start=False, stop=True, skip_group_check=True).then_inc(S["agg_mm"], 1)
        edges.close()
        with nc.Block() as last:
            @last.sync
            def _(sp):
                for s in (*S.values(), *rin):
                    sp.sem_clear(s)


def tile(ap, t):
    return ap[:, ds(t, 1), :].rearrange("p a d -> p (a d)")


class Stage:

    def __init__(self, nc, P, tag, sems):
        self.nc, self.tag, self.ctx, self.sems = nc, tag, ExitStack(), P["sems"]
        self.S = {n: self.sem(n) for n in sems.split()}

    def sem(self, name):
        return self.ctx.enter_context(self.nc.semaphore(f"{self.tag}_{name}"))

    def kept_sem(self, name):
        return self.sems.enter_context(self.nc.semaphore(f"{self.tag}_{name}"))

    def __enter__(self):
        return self

    def __exit__(self, *a):
        self.ctx.close()

    def sb(self, name, shape, dt=F32):
        return self.ctx.enter_context(self.nc.sbuf_tensor(f"{self.tag}_{name}", shape, dt))

    def block(self):
        return self.nc.Block()


def update_atoms(nc, P, A, X, agg, PS, w1s, w1v, w2s, w2v):
    with Stage(nc, P, "upd", "w_in dve at_ok turned sT_ok o1_mm o1_ok x_ok ln_ok h_ok oc_ok o2_mm act pool at_seen") as st:
        S = st.S
        wa, wb = st.sb("wa", [64, 2, 128]), st.sb("wb", [128, 2, 128])
        at, sT = st.sb("at", [TN, PU, 4, 64]), st.sb("sT", [64, 2, 4, TN])
        o1, ea, rl = st.sb("o1", [128, NT, 4, TN]), st.sb("ea", [128, NT, TN]), st.sb("rl", [128, NT, TN])
        oc = st.sb("oc", [128, 2, 4 * TN])
        with st.block() as block:
            @block.sync
            def _(sp):
                sp.dma_start(wa[:, 0, :], w1s).then_inc(S["w_in"], 16)
                sp.dma_start(wa[:, 1, :], w1v).then_inc(S["w_in"], 16)
                sp.dma_start(wb[:, 0, :], w2s).then_inc(S["w_in"], 16)
                sp.dma_start(wb[:, 1, :], w2v).then_inc(S["w_in"], 16)

            @block.gpsimd
            def _(pool):
                step = Steps(pool, S["pool"])
                for t in range(NT):
                    step.mark(pool.tensor_tensor(A[:, t, t * TN:(t + 1) * TN], A[:, t, t * TN:(t + 1) * TN], P["ident"][0:TN, 0:TN], ALU.add))
                step.wait()
                step(pool.tensor_tensor(P["asum"][0:TN, :], A[:, 0, :], A[:, 1, :], ALU.add))
                for t in range(2, NT):
                    step(pool.tensor_tensor(P["asum"][0:TN, :], P["asum"][0:TN, :], A[:, t, :], ALU.add))

            @block.vector
            def _(dve):
                step = Steps(dve, S["dve"])
                step(dve.tensor_tensor(agg[:, :, 160:192], agg[:, :, 160:192], agg[:, :, 224:256], ALU.add))
                step(dve.tensor_tensor(agg[:, :, 160:192], agg[:, :, 160:192], agg[:, :, 288:320], ALU.add))
                step(dve.tensor_scalar(agg[:, :, 160:192], agg[:, :, 160:192], IS3, None, ALU.mult))
                with dve.Fori(0, NT // PU) as i:
                    for k in range(PU):
                        dve.wait_ge(S["turned"], i * PU + (k + 1))
                        a = agg[:, ds(i * PU + k, 1), :].rearrange("p a (b f) -> p (a b) f", f=32)
                        dve.tensor_copy(at[:, k, 0, :].rearrange("p (b f) -> p b f", b=2), a[:, 0:6:5, :])
                        dve.tensor_copy(at[:, k, 1:4, 0:32], a[:, 4:9:2, :])
                        dve.tensor_copy(at[:, k, 1:4, 32:64], a[:, 1:4, :]).then_inc(S["at_ok"], 1)
                    for k in range(PU):
                        dve.wait_ge(S["o1_mm"], i * PU + (k + 1))
                        dve.tensor_scalar(o1[:, ds(i * PU + k, 1), :, :].rearrange("p a b n -> p (a b n)"), PS[:, 2 + k % 2, 0:4 * TN], 1.0 / 8.0, None, ALU.mult).then_inc(S["o1_ok"], 1)
                dve.wait_ge(S["o1_ok"], NT)
                step.mark(dve.tensor_scalar(rl[:, :, :], o1[:, :, 0, :], 0.0, -LOG2, ALU.max, ALU.add))
                step.wait()
                dve.wait_ge(S["ln_ok"], 1)
                dve.tensor_tensor(o1[:, :, 0, :], rl[:, :, :], ea[:, :, :], ALU.add).then_inc(S["h_ok"], 1)
                with dve.Fori(0, NT // 2) as i:
                    for k in range(2):
                        dve.wait_ge(S["o2_mm"], i * 2 + (k + 3))
                        x = tile(X, i * 2 + k)
                        dve.scalar_tensor_tensor(out=x[:, 0:128], in0=PS[0:TN, 4 + k, 0:128], scalar=1.0 / math.sqrt(B), in1=x[:, 0:128], op0=ALU.mult, op1=ALU.add)
                        xv = x[:, 128:D].rearrange("p (f c) -> p c f", c=3)
                        dve.scalar_tensor_tensor(out=xv, in0=PS[0:TN, 4 + k, 128:D].rearrange("p (c f) -> p c f", c=3), scalar=1.0 / math.sqrt(B), in1=xv, op0=ALU.mult, op1=ALU.add).then_inc(S["x_ok"], 1)
                        dve.wait_ge(S["x_ok"], i * 2 + (k + 3))
                        dve.bn_stats(tile(P["stats"], i * 2 + k), x)

            @block.scalar
            def _(act):
                act.sem_inc(S["sT_ok"], 2)
                with act.Fori(0, NT // PU) as i:
                    for k in range(PU):
                        act.wait_ge(S["turned"], i * PU + (k + PU + 1))
                        act.activation(sT[:, k % 2, :, :].rearrange("p b n -> p (b n)"), PS[0:64, k % 2, 0:4 * TN], ACT.Copy).then_inc(S["sT_ok"], 1)
                act.wait_ge(S["o1_ok"], NT)
                step = Steps(act, S["act"])
                step(act.activation(ea[:, :, :], o1[:, :, 0, :], ACT.Abs))
                step(act.activation(ea[:, :, :], ea[:, :, :], ACT.Exp, scale=-1.0))
                act.activation(ea[:, :, :], ea[:, :, :], ACT.Ln, bias=P["ones"][:, 0:1]).then_inc(S["ln_ok"], 1)
                act.wait_ge(S["h_ok"], 1)
                with act.Fori(0, NT // 2) as i:
                    for k in range(2):
                        act.wait_ge(S["o2_mm"], i * 2 + (k + 1))
                        act.activation(oc[:, k, :], o1[:, ds(i * 2 + k, 1), :, :].rearrange("p a b n -> p (a b n)"), ACT.Copy).then_inc(S["oc_ok"], 1)

            @block.tensor
            def _(pe):
                pe.wait_ge(S["w_in"], 64)
                pe.sem_inc(S["turned"], PU)
                pe.sem_inc(S["o2_mm"], 2)
                pe.sem_inc(S["x_ok"], 2)

                def turn(k, i):
                    pe.wait_ge(S["at_ok"], i * PU + (k + 1))
                    pe.sem_inc(S["at_seen"], 1)
                    for b in range(4):
                        ins = pe.transpose(PS[0:64, k % 2, b * TN:(b + 1) * TN], at[:, k, b, :], P["ident"][0:TN, 0:TN])
                    ins.then_inc(S["turned"], 1)

                def first_layer(i, k, first):
                    if k < PU - 1:
                        turn(k + 1, i)
                    pe.wait_ge(S["sT_ok"], i * PU + (k + 3))
                    if not (first and k < 2):
                        pe.wait_ge(S["o1_ok"], i * PU + (k - 1 if k else 0))
                    pe.matmul(PS[:, 2 + k % 2, 0:TN], wa[:, 0, :], sT[:, k % 2, 0, :], start=True, stop=True)
                    pe.matmul(PS[:, 2 + k % 2, TN:4 * TN], wa[:, 1, :], sT[:, k % 2, 1:4, :].rearrange("p b n -> p (b n)"), start=True, stop=True).then_inc(S["o1_mm"], 1)

                for i, first in ((0, True), (1, False)):
                    turn(0, i)
                    for k in range(PU):
                        first_layer(i, k, first)
                with pe.Fori(0, NT // 2) as i:
                    for k in range(2):
                        pe.wait_ge(S["oc_ok"], i * 2 + (k + 1))
                        pe.wait_ge(S["x_ok"], i * 2 + (k + 1))
                        for b in range(4):
                            ins = pe.matmul(PS[0:TN, 4 + k, b * 128:(b + 1) * 128], oc[:, k, b * TN:(b + 1) * TN], wb[:, min(b, 1), :], start=True, stop=True)
                        ins.then_inc(S["o2_mm"], 1)


def project(nc, tag, P, X, XH, PS, w, width, bias, scale, out, loads, w_in, w_at, later=()):
    with Stage(nc, P, tag, "dve var_ok std_ok xn_ready turned xs_ready mm out_ok") as st:
        S = st.S
        stats, mv = P["stats"], st.sb("mv", [TN, NT, 2])
        var, rstd, rtmp = st.sb("var", [TN, NT]), st.sb("rstd", [TN, NT]), st.sb("rtmp", [TN, NT])
        xn, xs = st.sb("xn", [TN, PU, D]), st.sb("xs", [128, PU, KC * TN])
        with st.block() as block:
            @block.sync
            def _(sp):
                for dst, src in loads:
                    sp.dma_start(dst, src).then_inc(w_in, 16)
                for dst, src, signal in later:
                    sp.dma_start(dst, src).then_inc(signal, 16)

            @block.vector
            def _(dve):
                step = Steps(dve, S["dve"])
                for t in range(NT):
                    step.mark(dve.bn_aggr(mv[:, t, :], stats[:, t, :]))
                step.wait()
                step(dve.tensor_scalar(var[:, :], mv[:, :, 1], 1e-5, None, ALU.add))
                dve.sem_inc(S["var_ok"], 1)
                dve.wait_ge(S["std_ok"], 1)
                step(dve.reciprocal(rstd[:, :], rstd[:, :]))
                step(dve.tensor_tensor(rtmp[:, :], rstd[:, :], rstd[:, :], ALU.mult))
                step(dve.tensor_tensor(rtmp[:, :], rtmp[:, :], var[:, :], ALU.mult))
                step(dve.tensor_scalar(rtmp[:, :], rtmp[:, :], -0.5, 1.5, ALU.mult, ALU.add))
                step(dve.tensor_tensor(rstd[:, :], rstd[:, :], rtmp[:, :], ALU.mult))

                with dve.Fori(0, NT // PU) as i:
                    for k in range(PU):
                        dve.wait_ge(S["turned"], i * PU + (k + 1))
                        dve.tensor_scalar(xn[:, k, :], tile(X, i * PU + k), tile(mv, i * PU + k)[:, 0:1], rstd[:, ds(i * PU + k, 1)], ALU.subtract, ALU.mult).then_inc(S["xn_ready"], 1)
                        if XH is not None:
                            dve.tensor_scalar(tile(XH, i * PU + k), tile(X, i * PU + k), tile(mv, i * PU + k)[:, 0:1], rstd[:, ds(i * PU + k, 1)], ALU.subtract, ALU.mult)
                    for k in range(PU):
                        dve.wait_ge(S["mm"], i * PU + (k + PU + 1))
                        if bias is not None:
                            dve.tensor_tensor(tile(out, i * PU + k), PS[0:TN, 2 + k, 0:width], bias, ALU.add).then_inc(S["out_ok"], 1)
                        elif scale is None:
                            dve.tensor_copy(tile(out, i * PU + k), PS[0:TN, 2 + k, 0:width]).then_inc(S["out_ok"], 1)
                        else:
                            dve.tensor_scalar(tile(out, i * PU + k), PS[0:TN, 2 + k, 0:width], scale[:, ds(i * PU + k, 1)], None, ALU.mult).then_inc(S["out_ok"], 1)
                dve.wait_ge(S["out_ok"], PU + NT)

            @block.scalar
            def _(act):
                act.wait_ge(S["var_ok"], 1)
                act.activation(rstd[:, :], var[:, :], ACT.Sqrt).then_inc(S["std_ok"], 1)
                with act.Fori(0, NT // PU) as i:
                    for k in range(PU):
                        act.wait_ge(S["turned"], i * PU + (k + PU + 1))
                        act.wait_ge(S["mm"], i * PU + (k + 1))
                        act.activation(xs[:, k, :], PS[:, k % 2, 0:KC * TN], ACT.Copy).then_inc(S["xs_ready"], 1)

            @block.tensor
            def _(pe):
                pe.wait_ge(w_in, w_at)
                pe.sem_inc(S["turned"], PU)
                pe.sem_inc(S["mm"], PU)
                pe.sem_inc(S["out_ok"], PU)

                def turn(k, i):
                    pe.wait_ge(S["xn_ready"], i * PU + (k + 1))
                    for c in range(KC):
                        ins = pe.transpose(PS[:, k % 2, c * TN:(c + 1) * TN], xn[:, k, c * 128:(c + 1) * 128], P["ident"][0:TN, 0:TN])
                    ins.then_inc(S["turned"], 1)

                with pe.Fori(0, NT // PU) as i:
                    turn(0, i)
                    for k in range(PU):
                        if k < PU - 1:
                            turn(k + 1, i)
                        pe.wait_ge(S["xs_ready"], i * PU + (k + 1))
                        pe.wait_ge(S["out_ok"], i * PU + (k + 1))
                        for c in range(KC):
                            ins = pe.matmul(PS[0:TN, 2 + k, 0:width], xs[:, k, c * TN:(c + 1) * TN], w[:, c, 0:width], start=(c == 0), stop=(c == KC - 1))
                        ins.then_inc(S["mm"], 1)


def pick_first(dve, step, lg, rev, mx, cand, oh, ms):
    step(dve.tensor_reduce(out=mx[:, :], in_=lg[:, :, :], axis=AX.X, op=ALU.max))
    bc = lambda a: a[:, :].rearrange("p (t a) -> p t a", a=1).broadcast_to([TN, NT, NX])
    step(dve.tensor_tensor(cand[:, :, :], lg[:, :, :], bc(mx), ALU.is_ge))
    step(dve.tensor_tensor(cand[:, :, :], cand[:, :, :], rev[:, :, :], ALU.mult))
    step(dve.tensor_reduce(out=ms[:, :], in_=cand[:, :, :], axis=AX.X, op=ALU.max))
    step(dve.tensor_tensor(oh[:, :, :], rev[:, :, :], bc(ms), ALU.is_equal))


def places(dve, pe_ok, step, PS, cum):
    pe_ok()
    step(dve.tensor_copy(cum[:, 0, :], PS[0:TN, 0, 0:NX]))
    run = cum[:, NT, :]
    step(dve.tensor_copy(run, PS[0:TN, 1, 0:NX]))
    for t in range(1, NT):
        step(dve.tensor_tensor(cum[:, t, :], PS[0:TN, 0, t * NX:(t + 1) * NX], run, ALU.add))
        step(dve.tensor_tensor(run, run, PS[0:TN, 1, t * NX:(t + 1) * NX], ALU.add))


def switch(nc, P, X, XH, PS, lg, ew, eb, xb, yb, dis, disb):
    with Stage(nc, P, "sw", "deg deg_mm sq sq_ok diag_ok bc_mm dve rev_ok oh_ok cum_mm sub_ok exp_ok to_ok eb_in xT xT_ok y_mm y_ok g_ok") as st:
        S = st.S
        S["sent"] = st.kept_sem("sent")
        win = [st.sem(f"win{r}") for r in range(4)]
        xin = [st.sem(f"xin{r}") for r in range(4)]
        yout = [st.sem(f"yout{r}") for r in range(4)]
        gin = [st.kept_sem(f"gin{r}") for r in range(NT)]
        rev, oh, cand, cum = st.sb("rev", [TN, NT, NX]), st.sb("oh", [TN, NT, NX]), st.sb("cand", [TN, NT, NX]), st.sb("cum", [TN, NT + 1, NX])
        mx, ms, prob, pos, rt, keep, t0, t1 = [st.sb(n, [TN, NT]) for n in "mx ms prob pos rt keep t0 t1".split()]
        dg, dr, dd = st.sb("dg", [TN, NT]), st.sb("dr", [TN, NT]), st.sb("dd", [TN, NT, TN])
        tok, toi, fri = st.sb("tok", [TN, NT]), st.sb("toi", [TN, NT], I32), st.sb("fri", [TN, NT], I32)
        we, ebr = st.sb("we", [128, 4, KC, D]), st.sb("ebr", [CAP, 4, D])
        xbs, xbT, ybs = st.sb("xbs", [CAP, 4, D]), st.sb("xbT", [128, 2, KC * CAP]), st.sb("ybs", [CAP, 4, D])
        bc = lambda a: a[:, :].rearrange("p (t a) -> p t a", a=1).broadcast_to([TN, NT, NX])
        with st.block() as block:
            @block.sync
            def _(sp):
                for r in range(4):
                    sp.dma_start(we[:, r, :, :], ew[r, :, :, :]).then_inc(win[r], 16)
                    sp.dma_start(ebr[:, r, :], eb[r:r + 1, :].broadcast_to([CAP, D])).then_inc(win[r], 16)

            @block.gpsimd
            def _(pool):
                pool.iota(rev[:, :, :], [[0, NT], [-1, NX]], base=NX, channel_multiplier=0, allow_small_or_imprecise_dtypes=True).then_inc(S["rev_ok"], 1)
                pool.iota(tok[:, :], [[TN, NT]], base=NX * CAP, channel_multiplier=1, allow_small_or_imprecise_dtypes=True).then_inc(S["rev_ok"], 1)
                pool.wait_ge(S["to_ok"], 1)
                for t in range(NT):
                    pool.indirect_dma_start(out=xb, out_offset=bass.IndirectOffsetOnAxis(ap=toi[:, t:t + 1], axis=0), in_=XH[:, t, :], in_offset=None).then_inc(S["sent"], 16)
                pool.wait_ge(S["sent"], 16 * NT)

            @block.vector
            def _(dve):
                step = Steps(dve, S["dve"])
                dve.wait_ge(S["rev_ok"], 2)
                pick_first(dve, step, lg, rev, mx, cand, oh, ms)
                dve.sem_inc(S["oh_ok"], 1)
                step(dve.tensor_tensor(cand[:, :, :], lg[:, :, :], bc(mx), ALU.subtract))
                dve.sem_inc(S["sub_ok"], 1)
                step(dve.tensor_scalar(rt[:, :], ms[:, :], -1.0, float(NX), ALU.mult, ALU.add))
                places(dve, lambda: dve.wait_ge(S["cum_mm"], 1), step, PS, cum)
                step(dve.tensor_tensor(oh[:, :, :], oh[:, :, :], cum[:, 0:NT, :], ALU.mult))
                step(dve.tensor_reduce(out=pos[:, :], in_=oh[:, :, :], axis=AX.X, op=ALU.add))
                step.mark(dve.tensor_scalar(keep[:, :], pos[:, :], float(CAP), None, ALU.is_lt))
                step(dve.tensor_scalar(t0[:, :], pos[:, :], float(CAP - 1), None, ALU.min))
                step(dve.scalar_tensor_tensor(out=t0[:, :], in0=rt[:, :], scalar=float(CAP), in1=t0[:, :], op0=ALU.mult, op1=ALU.add))
                step.mark(dve.tensor_copy(fri[:, :], t0[:, :]))
                step(dve.tensor_tensor(t1[:, :], t0[:, :], tok[:, :], ALU.subtract))
                step(dve.tensor_tensor(t1[:, :], t1[:, :], keep[:, :], ALU.mult))
                step(dve.tensor_tensor(t1[:, :], t1[:, :], tok[:, :], ALU.add))
                step(dve.tensor_copy(toi[:, :], t1[:, :]))
                dve.sem_inc(S["to_ok"], 1)
                dve.wait_ge(S["exp_ok"], 1)
                step(dve.tensor_reduce(out=prob[:, :], in_=cand[:, :, :], axis=AX.X, op=ALU.add))
                step(dve.reciprocal(prob[:, :], prob[:, :]))
                step(dve.tensor_tensor(t0[:, :], prob[:, :], keep[:, :], ALU.mult))
                step(dve.tensor_tensor(t1[:, :], prob[:, :], t0[:, :], ALU.subtract))
                for t in range(NT):
                    step.mark(dve.scalar_tensor_tensor(out=X[:, t, :], in0=XH[:, t, :], scalar=t1[:, t:t + 1], in1=X[:, t, :], op0=ALU.mult, op1=ALU.add))
                step.wait()
                step = Steps(dve, S["deg"])
                dve.wait_ge(S["deg_mm"], 1)
                step(dve.tensor_scalar(dg[:, :], PS[0:TN, 2, 0:NT], 1.0, None, ALU.max))
                dve.sem_inc(S["sq"], 1)
                dve.wait_ge(S["sq_ok"], 1)
                step(dve.reciprocal(dis[:, :], dis[:, :]))
                step(dve.tensor_tensor(dr[:, :], dis[:, :], dis[:, :], ALU.mult))
                step(dve.tensor_tensor(dr[:, :], dr[:, :], dg[:, :], ALU.mult))
                step(dve.tensor_scalar(dr[:, :], dr[:, :], -0.5, 1.5, ALU.mult, ALU.add))
                step(dve.tensor_tensor(dis[:, :], dis[:, :], dr[:, :], ALU.mult))
                step(dve.tensor_tensor(dd[:, :, :], P["ident"][0:TN, 0:TN].rearrange("p (a n) -> p a n", a=1).broadcast_to([TN, NT, TN]),
                                       dis[:, :].rearrange("p (t a) -> p t a", a=1).broadcast_to([TN, NT, TN]), ALU.mult))
                dve.sem_inc(S["diag_ok"], 1)
                dve.wait_ge(S["bc_mm"], 1)
                for q, n in enumerate((500, 500, 250)):
                    dve.tensor_copy(disb[:, 500 * q:500 * q + n], PS[:, 3 + q, 0:n])

            @block.scalar
            def _(act):
                act.wait_ge(S["sub_ok"], 1)
                act.activation(cand[:, :, :], cand[:, :, :], ACT.Exp).then_inc(S["exp_ok"], 1)
                act.wait_ge(S["sq"], 1)
                act.activation(dis[:, :], dg[:, :], ACT.Sqrt).then_inc(S["sq_ok"], 1)

            @block.tensor
            def _(pe):
                pe.wait_ge(S["oh_ok"], 1)
                o = oh[:, :, :].rearrange("p t e -> p (t e)")
                pe.matmul(PS[0:TN, 0, 0:NT * NX], P["before"][0:TN, 0:TN], o, start=True, stop=True)
                pe.matmul(PS[0:TN, 1, 0:NT * NX], P["ones"][0:TN, 0:TN], o, start=True, stop=True).then_inc(S["cum_mm"], 1)
                for t in range(NT):
                    ins = pe.matmul(PS[0:TN, 2, t:t + 1], P["asum"][0:TN, t * TN:(t + 1) * TN], P["ones"][0:TN, 0:1], start=True, stop=True)
                ins.then_inc(S["deg_mm"], 1)
                pe.wait_ge(S["diag_ok"], 1)
                d2 = dd[:, :, :].rearrange("p t n -> p (t n)")
                for q, n in enumerate((500, 500, 250)):
                    ins = pe.matmul(PS[:, 3 + q, 0:n], P["ones"][0:TN, :], d2[:, 500 * q:500 * q + n], start=True, stop=True)
                ins.then_inc(S["bc_mm"], 1)
        with st.block() as block:
            @block.sync
            def _(sp):
                with sp.Fori(1, NX // 4) as i:
                    for r in range(4):
                        sp.wait_ge(S["y_ok"], i * 4 + (r - 3))
                        sp.dma_start(we[:, r, :, :], ew[ds(i * 4 + r, 1), :, :, :].rearrange("a p k n -> p (a k) n")).then_inc(win[r], 16)
                        sp.dma_start(ebr[:, r, :], eb[ds(i * 4 + r, 1), :].broadcast_to([CAP, D])).then_inc(win[r], 16)

            @block.scalar
            def _(act):
                def store(r, i):
                    act.wait_ge(S["y_ok"], i * 4 + (r + 1))
                    act.dma_start(yb[ds((i * 4 + r) * CAP, CAP), :], ybs[:, r, :]).then_inc(yout[r], 16)

                for r in range(4):
                    act.dma_start(xbs[:, r, :], xb[r * CAP:(r + 1) * CAP, :]).then_inc(xin[r], 16)
                with act.Fori(0, NX // 4 - 1) as i:
                    for r in range(4):
                        store(r, i)
                        act.wait_ge(S["xT"], i * 4 + (r + 1))
                        act.dma_start(xbs[:, r, :], xb[ds((i * 4 + r + 4) * CAP, CAP), :]).then_inc(xin[r], 16)
                for r in range(4):
                    store(r, NX // 4 - 1)
                for r in range(4):
                    act.wait_ge(yout[r], 16 * (NX // 4))

            @block.vector
            def _(dve):
                def turned(r, i):
                    dve.wait_ge(S["xT"], i * 4 + (r + 1))
                    dve.tensor_copy(xbT[:, r % 2, :], PS[:, r % 2, 0:KC * CAP]).then_inc(S["xT_ok"], 1)

                def rows(i, first):
                    turned(0, i)
                    for r in range(4):
                        if r < 3:
                            turned(r + 1, i)
                        dve.wait_ge(S["y_mm"], i * 4 + (r + 1))
                        if not first:
                            dve.wait_ge(yout[r], i * 16)
                        dve.tensor_tensor(ybs[:, r, :], PS[0:CAP, 2 + r % 2, :], ebr[:, r, :], ALU.add).then_inc(S["y_ok"], 1)
                rows(0, True)
                with dve.Fori(1, NX // 4) as i:
                    rows(i, False)

            @block.tensor
            def _(pe):
                def turn(r, i):
                    pe.wait_ge(xin[r], i * 16 + 16)
                    for c in range(KC):
                        ins = pe.transpose(PS[:, r % 2, c * CAP:(c + 1) * CAP], xbs[:, r, c * 128:(c + 1) * 128], P["ident"][0:CAP, 0:CAP])
                    ins.then_inc(S["xT"], 1)

                with pe.Fori(0, NX // 4) as i:
                    turn(0, i)
                    for r in range(4):
                        if r < 3:
                            turn(r + 1, i)
                        pe.wait_ge(win[r], i * 32 + 32)
                        pe.wait_ge(S["xT_ok"], i * 4 + (r + 1))
                        for c in range(KC):
                            ins = pe.matmul(PS[0:CAP, 2 + r % 2, :], xbT[:, r % 2, c * CAP:(c + 1) * CAP], we[:, r, c, :], start=(c == 0), stop=(c == KC - 1))
                        ins.then_inc(S["y_mm"], 1)
        with st.block() as block:
            gg = we[0:TN, :, :, :].rearrange("p r k n -> p (r k) n")
            @block.gpsimd
            def _(pool):
                for t in range(NT):
                    pool.indirect_dma_start(out=gg[:, t, :], out_offset=None, in_=yb, in_offset=bass.IndirectOffsetOnAxis(ap=fri[:, t:t + 1], axis=0)).then_inc(gin[t], 16)

            @block.vector
            def _(dve):
                step = Steps(dve, S["g_ok"])
                for t in range(NT):
                    dve.wait_ge(gin[t], 16)
                    step.mark(dve.scalar_tensor_tensor(out=X[:, t, :], in0=gg[:, t, :], scalar=t0[:, t:t + 1], in1=X[:, t, :], op0=ALU.mult, op1=ALU.add))
                    if t >= 1:
                        dve.wait_ge(S["g_ok"], t)
                        dve.bn_stats(P["stats"][:, t - 1, :], X[:, t - 1, :])
                step.wait()
                dve.bn_stats(P["stats"][:, NT - 1, :], X[:, NT - 1, :])


def convolve(nc, P, A, X, PS, hs, hs2, dis, disb, w2, b1c, b2r):
    with Stage(nc, P, "conv", "agg_mm u_ok h_ok p_mm p_ok a_ok o_mm b_ok x_ok") as st:
        S = st.S
        u, hT = st.sb("u", [128, 2, 250]), st.sb("hT", [128, KC, 250])
        Ac = st.sb("Ac", [TN, 2, NT, TN])
        with st.block() as block:
            @block.tensor
            def _(pe):
                pe.sem_inc(S["u_ok"], 2)
                pe.sem_inc(S["p_ok"], 2)
                with pe.Fori(0, NT // 2) as i:
                    for c in range(KC):
                        pe.wait_ge(S["u_ok"], i * KC + (c + 1))
                        for s in range(NT):
                            ins = pe.matmul(PS[:, c % 2, 0:250], hs[:, s, c * 128:(c + 1) * 128], A[:, s, ds(i * 250, 250)], start=(s == 0), stop=(s == NT - 1))
                        ins.then_inc(S["agg_mm"], 1)
                    pe.wait_ge(S["h_ok"], i * KC + (KC + 2))
                    for q in range(2):
                        pe.wait_ge(S["p_ok"], i * 2 + (q + 1))
                        for c in range(KC):
                            ins = pe.matmul(PS[0:TN, 2 + q, :], hT[:, c, q * TN:(q + 1) * TN], w2[:, c, :], start=(c == 0), stop=(c == KC - 1))
                        ins.then_inc(S["p_mm"], 1)

            @block.vector
            def _(dve):
                with dve.Fori(0, NT // 2) as i:
                    for c in range(KC):
                        dve.wait_ge(S["agg_mm"], i * KC + (c + 1))
                        dve.wait_ge(S["h_ok"], i * KC + (c + 1))
                        dve.tensor_tensor(u[:, c % 2, :], PS[:, c % 2, 0:250], disb[:, ds(i * 250, 250)], ALU.mult).then_inc(S["u_ok"], 1)
                    for q in range(2):
                        dve.wait_ge(S["p_mm"], i * 2 + (q + 1))
                        dve.tensor_scalar(tile(hs2, i * 2 + q), PS[0:TN, 2 + q, :], dis[:, ds(i * 2 + q, 1)], None, ALU.mult).then_inc(S["p_ok"], 1)
                dve.wait_ge(S["p_ok"], 2 + NT)

            @block.scalar
            def _(act):
                act.sem_inc(S["h_ok"], 2)

                def hidden(i, first):
                    for c in range(KC):
                        act.wait_ge(S["u_ok"], i * KC + (c + 3))
                        if not first:
                            act.wait_ge(S["p_mm"], i * 2)
                        act.activation(hT[:, c, :], u[:, c % 2, :], ACT.Relu, bias=b1c[:, c:c + 1]).then_inc(S["h_ok"], 1)

                hidden(0, True)
                with act.Fori(1, NT // 2) as i:
                    hidden(i, False)

            @block.gpsimd
            def _(pool):
                pool.tensor_tensor(X[:, :, :], X[:, :, :], b2r[:, :].rearrange("p (a d) -> p a d", a=1).broadcast_to([TN, NT, D]), ALU.add).then_inc(S["b_ok"], 1)
                pool.wait_ge(S["b_ok"], 1)
        with st.block() as block:
            @block.scalar
            def _(act):
                act.sem_inc(S["o_mm"], 2)
                with act.Fori(0, NT // 2) as i:
                    for k in range(2):
                        act.wait_ge(S["o_mm"], i * 2 + (k + 1))
                        act.activation(Ac[:, k, :, :], A[:, :, ds((i * 2 + k) * TN, TN)], ACT.Copy).then_inc(S["a_ok"], 1)

            @block.tensor
            def _(pe):
                pe.sem_inc(S["x_ok"], 2)
                with pe.Fori(0, NT // 2) as i:
                    for k in range(2):
                        pe.wait_ge(S["a_ok"], i * 2 + (k + 1))
                        pe.wait_ge(S["x_ok"], i * 2 + (k + 1))
                        for s in range(NT):
                            ins = pe.matmul(PS[0:TN, k, :], Ac[:, k, s, :], hs2[:, s, :], start=(s == 0), stop=(s == NT - 1))
                        ins.then_inc(S["o_mm"], 1)

            @block.vector
            def _(dve):
                with dve.Fori(0, NT // 2) as i:
                    for k in range(2):
                        dve.wait_ge(S["o_mm"], i * 2 + (k + 3))
                        x = tile(X, i * 2 + k)
                        dve.scalar_tensor_tensor(out=x, in0=PS[0:TN, k, :], scalar=dis[:, ds(i * 2 + k, 1)], in1=x, op0=ALU.mult, op1=ALU.add).then_inc(S["x_ok"], 1)
                        dve.wait_ge(S["x_ok"], i * 2 + (k + 3))
                        dve.bn_stats(tile(P["stats"], i * 2 + k), x)


def mixture(nc, P, X, XH, PS, lg, w1, w1_in, w2t, xb, out):
    with Stage(nc, P, "mix", "dve dve2 rev_ok oh_ok cum_mm sub_ok exp_ok to_ok w2_in meta_ok xT xT_ok h_mm s_ok sum_mm mean_ok y_mm y_ok rT rT_ok o_mm x_ok out_ok") as st:
        S = st.S
        S["sent"] = st.kept_sem("sent")
        xin = [st.sem(f"xin{r}") for r in range(JU)]
        rev = st.sb("rev", [TN, NT, NX])
        l2, cand, cum, both = st.sb("l2", [TN, NT, NX]), st.sb("cand", [TN, NT, NX]), st.sb("cum", [TN, NT + 1, NX]), st.sb("both", [TN, NT, NX])
        oh = st.sb("oh", [TN, 2, NT, NX])
        mx, ms, wt, dst = st.sb("mx", [TN, 2, NT]), st.sb("ms", [TN, NT]), st.sb("wt", [TN, 2, NT]), st.sb("dst", [TN, 2, NT])
        dsti = st.sb("dsti", [TN, 2, NT], I32)
        c16, c16i, rc = st.sb("c16", [128, 6, NX]), st.sb("c16i", [128, 2, NX], I32), st.sb("rc", [128, NX])
        jx, onej, jm, sl = st.sb("jx", [128, JOBS]), st.sb("onej", [128, JOBS, NX]), st.sb("jm", [1, JOBS], I32), st.sb("sl", [128, JOBS])
        ji = st.sb("ji", [128, JOBS])
        e16, diag = st.sb("e16", [128, NX]), st.sb("diag", [128, NX, NX])
        xbs, xbT, hh = st.sb("xbs", [128, JU, D]), st.sb("xbT", [128, 2, D]), st.sb("hh", [128, 2, H1])
        zz, hm, hd = st.sb("zz", [128, 128]), st.sb("hm", [128, 2, NX]), st.sb("hd", [128, 2, NX, NX])
        ym, rT, w2 = st.sb("ym", [NX, D]), st.sb("rT", [NX, NT * TN]), st.sb("w2", [128, NX, 2, D])
        bc = lambda a: a.rearrange("p (t a) -> p t a", a=1).broadcast_to([TN, NT, NX])
        with st.block() as block:
            @block.sync
            def _(sp):
                sp.dma_start(w2[:, :, :, :], w2t).then_inc(S["w2_in"], 16)

            @block.gpsimd
            def _(pool):
                pool.iota(rev[:, :, :], [[0, NT], [-1, NX]], base=NX, channel_multiplier=0, allow_small_or_imprecise_dtypes=True).then_inc(S["rev_ok"], 1)
                pool.iota(ji[:, :], [[1, JOBS]], base=0, channel_multiplier=0, allow_small_or_imprecise_dtypes=True).then_inc(S["rev_ok"], 1)
                pool.iota(e16[:, :], [[1, NX]], base=0, channel_multiplier=0, allow_small_or_imprecise_dtypes=True).then_inc(S["rev_ok"], 1)
                pool.memset(zz[:, :], 0.0).then_inc(S["rev_ok"], 1)
                pool.wait_ge(S["to_ok"], 1)
                for k in range(2):
                    for t in range(NT):
                        pool.indirect_dma_start(out=xb, out_offset=bass.IndirectOffsetOnAxis(ap=dsti[:, k, t:t + 1], axis=0), in_=XH[:, t, :], in_offset=None).then_inc(S["sent"], 16)
                pool.wait_ge(S["sent"], 32 * NT)

            @block.vector
            def _(dve):
                step = Steps(dve, S["dve"])
                dve.wait_ge(S["rev_ok"], 4)
                pick_first(dve, step, lg, rev, mx[:, 0, :], cand, oh[:, 0, :, :], ms)
                step(dve.scalar_tensor_tensor(out=l2[:, :, :], in0=oh[:, 0, :, :], scalar=-1e30, in1=lg[:, :, :], op0=ALU.mult, op1=ALU.add))
                pick_first(dve, step, l2, rev, mx[:, 1, :], cand, oh[:, 1, :, :], ms)
                step(dve.tensor_tensor(both[:, :, :], oh[:, 0, :, :], oh[:, 1, :, :], ALU.add))
                dve.sem_inc(S["oh_ok"], 1)
                step(dve.tensor_tensor(wt[:, 1, :], mx[:, 1, :], mx[:, 0, :], ALU.subtract))
                dve.sem_inc(S["sub_ok"], 1)
                places(dve, lambda: dve.wait_ge(S["cum_mm"], 1), step, PS, cum)
                step(dve.tensor_copy(c16[:, 0, :], PS[:, 2, 0:NX]))
                step(dve.tensor_scalar(c16[:, 1, :], c16[:, 0, :], 127.0, None, ALU.add))
                step(dve.tensor_copy(c16i[:, 0, :], c16[:, 1, :]))
                step(dve.tensor_scalar(c16i[:, 1, :], c16i[:, 0, :], 7, None, ALU.arith_shift_right))
                step.mark(dve.memset(c16[:, 5, :], 0.0))
                step(dve.tensor_copy(c16[:, 2, :], c16i[:, 1, :]))
                step(dve.tensor_tensor_scan(out=c16[:, 3, :], data0=c16[:, 2, :], data1=c16[:, 5, :], initial=0.0, op0=ALU.add, op1=ALU.add))
                step(dve.tensor_tensor(c16[:, 4, :], c16[:, 3, :], c16[:, 2, :], ALU.subtract))
                step(dve.tensor_scalar(c16[:, 4, :], c16[:, 4, :], 128.0, None, ALU.mult))
                step(dve.tensor_tensor(cum[:, 0:NT, :], cum[:, 0:NT, :], c16[0:TN, 4:5, :].broadcast_to([TN, NT, NX]), ALU.add))
                for k in range(2):
                    step(dve.tensor_tensor(cand[:, :, :], oh[:, k, :, :], cum[:, 0:NT, :], ALU.mult))
                    step(dve.tensor_reduce(out=dst[:, k, :], in_=cand[:, :, :], axis=AX.X, op=ALU.add))
                step(dve.tensor_copy(dsti[:, :, :], dst[:, :, :]))
                dve.sem_inc(S["to_ok"], 1)
                step(dve.tensor_tensor(onej[:, :, :], ji[:, :].rearrange("p (j a) -> p j a", a=1).broadcast_to([128, JOBS, NX]),
                                       c16[:, 3:4, :].broadcast_to([128, JOBS, NX]), ALU.is_ge))
                step(dve.tensor_reduce(out=jx[:, :], in_=onej[:, :, :], axis=AX.X, op=ALU.add))
                step(dve.tensor_scalar(jx[:, :], jx[:, :], float(NX - 1), None, ALU.min))
                step.mark(dve.tensor_copy(jm[:, :], jx[0:1, :]))
                step(dve.tensor_tensor(onej[:, :, :], jx[:, :].rearrange("p (j a) -> p j a", a=1).broadcast_to([128, JOBS, NX]),
                                       e16[:, :].rearrange("p (a e) -> p a e", a=1).broadcast_to([128, JOBS, NX]), ALU.is_equal))
                step.mark(dve.tensor_tensor(diag[:, :, :], e16[:, :].rearrange("p (a e) -> p a e", a=1).broadcast_to([128, NX, NX]),
                                            e16[:, :].rearrange("p (e a) -> p e a", a=1).broadcast_to([128, NX, NX]), ALU.is_equal))
                step(dve.tensor_scalar(rc[:, :], c16[:, 0, :], 1.0, None, ALU.max))
                step(dve.reciprocal(rc[:, :], rc[:, :]))
                dve.wait_ge(S["exp_ok"], 1)
                step(dve.tensor_scalar(wt[:, 0, :], wt[:, 1, :], 1.0, None, ALU.add))
                step(dve.reciprocal(wt[:, 0, :], wt[:, 0, :]))
                step(dve.tensor_tensor(wt[:, 1, :], wt[:, 0, :], wt[:, 1, :], ALU.mult))
                step.mark(dve.tensor_tensor(both[:, :, :], oh[:, 0, :, :], bc(wt[:, 0, :]), ALU.mult))
                step(dve.tensor_tensor(cand[:, :, :], oh[:, 1, :, :], bc(wt[:, 1, :]), ALU.mult))
                step(dve.tensor_tensor(both[:, :, :], both[:, :, :], cand[:, :, :], ALU.add))

            @block.scalar
            def _(act):
                act.wait_ge(S["sub_ok"], 1)
                act.activation(wt[:, 1, :], wt[:, 1, :], ACT.Exp).then_inc(S["exp_ok"], 1)

            @block.tensor
            def _(pe):
                pe.wait_ge(S["oh_ok"], 1)
                o = both[:, :, :].rearrange("p t e -> p (t e)")
                pe.matmul(PS[0:TN, 0, 0:NT * NX], P["before"][0:TN, 0:TN], o, start=True, stop=True)
                pe.matmul(PS[0:TN, 1, 0:NT * NX], P["ones"][0:TN, 0:TN], o, start=True, stop=True)
                for t in range(NT):
                    ins = pe.matmul(PS[:, 2, 0:NX], P["ones"][0:TN, :], both[:, t, :], start=(t == 0), stop=(t == NT - 1))
                ins.then_inc(S["cum_mm"], 1)
        with st.block() as block:
            @block.sync
            def _(sp):
                sp.sem_inc(S["xT"], JU)
                with sp.Fori(0, JOBS // JU) as i:
                    for r in range(JU):
                        sp.wait_ge(S["xT"], i * JU + (r + 1))
                        sp.dma_start(xbs[:, r, :], xb[ds((i * JU + r) * 128, 128), :]).then_inc(xin[r], 16)

            @block.tensor
            def _(pe):
                pe.matmul(PS[:, 4, 0:2 * NX], zz[:, :], zz[:, 0:2 * NX], start=True, stop=True).then_inc(S["sum_mm"], 1)
                pe.sem_inc(S["sum_mm"], 2)
                pe.sem_inc(S["s_ok"], 1)
                pe.wait_ge(w1_in, 16)
                def turn(r, q, i):
                    pe.wait_ge(xin[r], i * 16 + 16)
                    for c in range(KC):
                        ins = pe.transpose(PS[:, q, c * 128:(c + 1) * 128], xbs[:, r, c * 128:(c + 1) * 128], P["ident"][:, :])
                    ins.then_inc(S["xT"], 1)

                def hidden(r, q, i):
                    e = pe.value_load(jm[0:1, ds(i * JU + r, 1)], min_val=0, max_val=NX - 1)
                    pe.wait_ge(S["xT_ok"], i * JU + (r + 1))
                    for c in range(KC):
                        ins = pe.matmul(PS[:, 2 + q, 0:H1], xbT[:, q, c * 128:(c + 1) * 128], w1[:, ds(e, 1), c, :].rearrange("p a n -> p (a n)"), start=(c == 0), stop=(c == KC - 1))
                    ins.then_inc(S["h_mm"], 1)

                def total(r, q, i):
                    pe.wait_ge(S["s_ok"], i * JU + (r + 2))
                    for f in range(2):
                        ins = pe.matmul(PS[:, 4, f * NX:(f + 1) * NX], hh[:, q, f * 128:(f + 1) * 128], onej[:, ds(i * JU + r, 1), :].rearrange("p a e -> p (a e)"), start=False, stop=True, skip_group_check=True)
                    ins.then_inc(S["sum_mm"], 1)

                with pe.Fori(0, JOBS // JU) as i:
                    turn(0, 0, i)
                    for r in range(JU):
                        if r < JU - 1:
                            turn(r + 1, (r + 1) % 2, i)
                        hidden(r, r % 2, i)
                        if r >= 1:
                            total(r - 1, (r - 1) % 2, i)
                    total(JU - 1, (JU - 1) % 2, i)
                pe.wait_ge(S["mean_ok"], 1)
                pe.wait_ge(S["w2_in"], 16)
                for e in range(NX):
                    for f in range(2):
                        ins = pe.matmul(PS[0:NX, 5, :], hd[:, f, e, :], w2[:, e, f, :], start=(e == 0 and f == 0), stop=(e == NX - 1 and f == 1))
                ins.then_inc(S["y_mm"], 1)
                for t in range(NT):
                    ins = pe.transpose(PS[0:NX, t // 4, (t % 4) * TN:(t % 4 + 1) * TN], both[:, t, :], P["ident"][0:TN, 0:TN])
                ins.then_inc(S["rT"], 1)
                pe.wait_ge(S["rT_ok"], 3)
                pe.wait_ge(S["y_ok"], 1)
                for t in range(NT):
                    if t >= 4:
                        pe.wait_ge(S["x_ok"], t - 3)
                    pe.matmul(PS[0:TN, t % 4, :], rT[:, t * TN:(t + 1) * TN], ym[:, :], start=True, stop=True).then_inc(S["o_mm"], 1)

            @block.vector
            def _(dve):
                with dve.Fori(0, JOBS // JU) as i:
                    for r in range(JU):
                        dve.wait_ge(S["xT"], i * JU + (r + 1 + JU))
                        dve.tensor_copy(xbT[:, r % 2, :], PS[:, r % 2, :]).then_inc(S["xT_ok"], 1)
                step = Steps(dve, S["dve2"])
                dve.wait_ge(S["sum_mm"], 3 + JOBS)
                step(dve.tensor_tensor(hm[:, :, :], PS[:, 4, 0:2 * NX].rearrange("p (f e) -> p f e", f=2), rc[:, :].rearrange("p (a e) -> p a e", a=1).broadcast_to([128, 2, NX]), ALU.mult))
                for f in range(2):
                    ins = dve.tensor_tensor(hd[:, f, :, :], diag[:, :, :],
                                            hm[:, f:f + 1, :].broadcast_to([128, NX, NX]), ALU.mult)
                    step.mark(ins)
                step.wait()
                dve.sem_inc(S["mean_ok"], 1)
                dve.wait_ge(S["rT"], 1)
                for q, n in enumerate((500, 500, 250)):
                    dve.tensor_copy(rT[:, 500 * q:500 * q + n], PS[0:NX, q, 0:n]).then_inc(S["rT_ok"], 1)
                dve.wait_ge(S["y_mm"], 1)
                dve.tensor_copy(ym[:, :], PS[0:NX, 5, :]).then_inc(S["y_ok"], 1)
                for t in range(NT):
                    dve.wait_ge(S["o_mm"], t + 1)
                    dve.tensor_tensor(X[:, t, :], PS[0:TN, t % 4, :], X[:, t, :], ALU.add).then_inc(S["x_ok"], 1)

            @block.scalar
            def _(act):
                with act.Fori(0, JOBS // JU) as i:
                    for r in range(JU):
                        act.wait_ge(S["h_mm"], i * JU + (r + 1))
                        act.wait_ge(S["sum_mm"], i * JU + (r + 2))
                        act.activation(hh[:, r % 2, :], PS[:, 2 + r % 2, 0:H1], ACT.Silu).then_inc(S["s_ok"], 1)
                for t in range(NT):
                    act.wait_ge(S["x_ok"], t + 1)
                    act.dma_start(out[t * TN:(t + 1) * TN, :], X[:, t, :]).then_inc(S["out_ok"], 16)
                act.wait_ge(S["out_ok"], 16 * NT)


def program(nc, x, fT_d, sm_d, ds_i, w2e, b2e, in2f_s, in2f_v, W1, b1, f1s, f1v, f2s, f2v, sw, swb, ew, eb, g1, g1b, g2, g2b, gate, w1, w2, out):
    xb0 = nc.dram_tensor("xb0", (NX * CAP + N, D), F32, kind="Internal").ap()
    yb0 = nc.dram_tensor("yb0", (NX * CAP, D), F32, kind="Internal").ap()
    xb1 = nc.dram_tensor("xb1", (JOBS * 128, D), F32, kind="Internal").ap()
    with ExitStack() as ctx:
        def sb(name, shape, dt=F32):
            return nc.sbuf_tensor(name, shape, dt)

        P = {n: ctx.enter_context(sb(n, [128, 128])) for n in ("ident", "ones", "before")}
        P["stats"] = ctx.enter_context(sb("xstats", [TN, NT, 6]))
        P["sems"] = ctx.enter_context(ExitStack())
        X = ctx.enter_context(sb("X", [TN, NT, D]))
        PS = ctx.enter_context(nc.psum_tensor("PS", [128, 8, 512], F32))
        sw_in, g_in, gate_in, w1_in = [ctx.enter_context(nc.semaphore(n)) for n in ("sw_in", "g_in", "gate_in", "w1_in_all")]
        with sb("A", [TN, NT, N]) as A, sb("asum", [128, N]) as asum, sb("dis", [TN, NT]) as dis, sb("disb", [128, N]) as disb:
            P["asum"] = asum
            with sb("agg", [TN, NT, 320]) as agg:
                edge_phase(nc, P, A, X, agg, PS, x, fT_d, sm_d, ds_i, w2e, b2e, in2f_s, in2f_v, W1, b1,
                           [xb0[0:NX * CAP, :].rearrange("(p q) d -> p q d", q=12), xb1.rearrange("(p q) d -> p q d", q=JOBS)])
                update_atoms(nc, P, A, X, agg, PS, f1s, f1v, f2s, f2v)
            with sb("XH0", [TN, NT, D]) as XH, sb("lg0", [TN, NT, NX]) as lg, sb("sww", [128, KC, NX]) as sww, sb("swbb", [TN, NX]) as swbb:
                project(nc, "p0", P, X, XH, PS, sww, NX, swbb[:, :], None, lg, ((sww[:, :, :], sw), (swbb[:, :], swb.broadcast_to([TN, NX]))), sw_in, 32)
                switch(nc, P, X, XH, PS, lg, ew, eb, xb0, yb0, dis, disb)
            with sb("hs", [TN, NT, D]) as hs, sb("hs2", [TN, NT, D]) as hs2, \
                    sb("g1w", [128, KC, D]) as g1w, sb("g2w", [128, KC, D]) as g2w, sb("g1bc", [128, KC]) as g1bc, sb("g2br", [TN, D]) as g2br:
                project(nc, "p1", P, X, None, PS, g1w, D, None, dis, hs,
                        ((g1w[:, :, :], g1), (g2w[:, :, :], g2), (g1bc[:, :], g1b), (g2br[:, :], g2b.broadcast_to([TN, D]))), g_in, 64)
                convolve(nc, P, A, X, PS, hs, hs2, dis, disb, g2w, g1bc, g2br)
        with sb("w1s", [128, NX, KC, H1]) as w1s, sb("XH1", [TN, NT, D]) as XH, sb("lg1", [TN, NT, NX]) as lg, sb("gw", [128, KC, NX]) as gw:
            project(nc, "p2", P, X, XH, PS, gw, NX, None, None, lg, ((gw[:, :, :], gate),), gate_in, 16, ((w1s[:, :, :, :], w1, w1_in),))
            mixture(nc, P, X, XH, PS, lg, w1s, w1_in, w2, xb1, out)


def kernel(**inputs):
    import numpy as np
    import concourse.bacc as bacc
    from concourse.bass_utils import run_bass_kernel_spmd

    I = {n: np.asarray(a) for n, a in inputs.items()}
    EP = NE * 128
    f = np.zeros((EP, R), np.float32)
    f[:E] = I["edge_attr_20"]
    y = np.zeros((EP, 5), np.float32)
    y[:E, :4] = I["edge_attr_4"]
    y[:E, 4] = I["edge_weight"]
    ends = np.zeros((2, EP), np.int32)
    ends[0, E:] = PAD
    ends[0, :E] = I["src"]
    ends[1, :E] = I["dst"]
    W2 = I["L0_gnn_W2"].reshape(F, F, 6).transpose(0, 2, 1)[:, (0, 3, 2, 1)].reshape(F, 4 * F)
    b2 = I["L0_gnn_b2"].reshape(F, 6).T[(0, 3, 2, 1), :].reshape(1, 4 * F)
    v1 = I["L0_gnn_w_f2o1_v"]
    chunks = lambda a: a.reshape(KC, 128, -1).transpose(1, 0, 2)
    arrays = dict(
        x=I["x"], f_t=f.reshape(NQ, 4, 128, R).transpose(1, 3, 0, 2).reshape(4 * R, NQ * 128), y_rcut=y.reshape(NE, 128, 5).transpose(1, 0, 2),
        ends=ends.reshape(2, NE, 128).transpose(2, 0, 1), w2e=W2, b2e=b2,
        in2f_s=I["L0_gnn_w_in2f_s"], in2f_v=I["L0_gnn_w_in2f_v"], rad_w1=I["L0_gnn_W1"], rad_b1=I["L0_gnn_b1"].reshape(F, 1),
        f2o1_s=I["L0_gnn_w_f2o1_s"], f2o1_v=v1, f2o2_s=I["L0_gnn_w_f2o2_s"], f2o2_v=I["L0_gnn_w_f2o2_v"],
        switch_w=chunks(I["L0_ffn_switch_w"].T), switch_b=I["L0_ffn_switch_b"].reshape(1, NX),
        expert_w=I["L0_ffn_expert_w"].transpose(0, 2, 1).reshape(NX, KC, 128, D).transpose(0, 2, 1, 3), expert_b=I["L0_ffn_expert_b"],
        g1=chunks(I["L1_gnn_W1"]), g1b=I["L1_gnn_b1"].reshape(KC, 128).T, g2=chunks(I["L1_gnn_W2"]), g2b=I["L1_gnn_b2"].reshape(1, D),
        gate=chunks(I["L1_ffn_gate_weight"].T), w1=I["L1_ffn_w1"].reshape(NX, H1, KC, 128).transpose(3, 0, 2, 1),
        w2=I["L1_ffn_w2"].reshape(NX, D, 2, 128).transpose(3, 0, 2, 1))
    nc = bacc.Bacc("TRN2", target_bir_lowering=False, num_devices=1)
    arrays = {f"{n}_d": np.ascontiguousarray(a) for n, a in arrays.items()}
    aps = [nc.dram_tensor(n, a.shape, mybir.dt.from_np(a.dtype), kind="ExternalInput").ap() for n, a in arrays.items()]
    out = nc.dram_tensor("out_d", (N, D), F32, kind="ExternalOutput").ap()
    program(nc, *aps, out)
    return run_bass_kernel_spmd(nc, [arrays], core_ids=[0]).results[0]["out_d"]
```
